# Optimizing a Trainium2 kernel written in Bass

```python
import numpy as np
import jax
import jax.numpy as jnp

def _softmax(x, axis=-1):
    return jax.nn.softmax(x, axis=axis)

def _gelu(x):
    return jax.nn.gelu(x, approximate=True)

def _silu(x):
    return jax.nn.silu(x)

def _sigmoid(x):
    return jax.nn.sigmoid(x)

def _layernorm(x, axis=-1, eps=1e-05):
    m = jnp.mean(x, axis=axis, keepdims=True)
    v = jnp.var(x, axis=axis, keepdims=True)
    return (x - m) / jnp.sqrt(v + eps)

def _scatter_add(tgt, idx, src, axis=0):
    return tgt.at[idx].add(src)

def _segment_sum(src, seg, n):
    return jax.ops.segment_sum(src, seg, n)
kernel_name = 'mk_prb_d2_jaxref_r8_d1d3a8'

def setup_inputs(seed: int=0):
    np.random.seed(seed)
    _w = jnp.asarray

    def _L0_attn_setup():
        import jax, jax.numpy as jnp
        import numpy as np
        B, T, D, R = (4, 256, 128, 64)
        key = jax.random.key(seed)
        ks = jax.random.split(key, 13)
        x = jax.random.normal(ks[0], (B, T, D), jnp.float32)
        WQ = jax.random.normal(ks[1], (D, D), jnp.float32) * 0.02
        WK = jax.random.normal(ks[2], (D, D), jnp.float32) * 0.02
        WO = jax.random.normal(ks[3], (D, D), jnp.float32) * 0.02
        Winv = jnp.eye(D, dtype=jnp.float32) + 0.01 * jax.random.normal(ks[4], (D, D), jnp.float32)
        U_b = jax.random.normal(ks[5], (D, R), jnp.float32) * 0.02
        V_b = jax.random.normal(ks[6], (D, R), jnp.float32) * 0.02
        W_b = jax.random.normal(ks[7], (D, R), jnp.float32) * 0.02
        bias_b = jnp.zeros((D,), jnp.float32)
        U_t = jax.random.normal(ks[8], (D, R), jnp.float32) * 0.02
        V_t = jax.random.normal(ks[9], (D, R), jnp.float32) * 0.02
        W_t = jax.random.normal(ks[10], (D, R), jnp.float32) * 0.02
        X_t = jax.random.normal(ks[11], (D, R), jnp.float32) * 0.02
        bias_t = jnp.zeros((D,), jnp.float32)
        alpha_bi = jnp.float32(0.5)
        alpha_tri = jnp.float32(0.5)
        return {'x': x, 'WQ': WQ, 'WK': WK, 'WO': WO, 'Winv': Winv, 'U_b': U_b, 'V_b': V_b, 'W_b': W_b, 'bias_b': bias_b, 'U_t': U_t, 'V_t': V_t, 'W_t': W_t, 'X_t': X_t, 'bias_t': bias_t, 'alpha_bi': alpha_bi, 'alpha_tri': alpha_tri}
    _L0_attn_in = _L0_attn_setup()

    def _L0_ffn_setup():
        import jax, jax.numpy as jnp
        import numpy as np
        D = 128
        H = 256
        E = 8
        K = 2
        B, T = (4, 256)
        key = jax.random.key(seed)
        ks = jax.random.split(key, 7)
        s = 0.02
        return {'x': jax.random.normal(ks[0], (B, T, D), dtype=jnp.float32), 'W1': jax.random.normal(ks[1], (E, D, 2 * H), dtype=jnp.float32) * s, 'b1': jnp.zeros((E, 2 * H), dtype=jnp.float32), 'W2': jax.random.normal(ks[2], (E, H, D), dtype=jnp.float32) * s, 'b2': jnp.zeros((E, D), dtype=jnp.float32), 'Wr': jax.random.normal(ks[3], (D, E), dtype=jnp.float32) * s, 'br': jnp.zeros((E,), dtype=jnp.float32)}
    _L0_ffn_in = _L0_ffn_setup()

    def _L1_attn_setup():
        import jax, jax.numpy as jnp
        import numpy as np
        BLOCK = 64
        NUM_GLOBAL = 16
        GBL = BLOCK // NUM_GLOBAL
        NEG = -10000.0
        E = 128
        H = 16

        def _sparse_attn(q, k, v, M):
            B, Hn, S, d = q.shape
            nb = S // BLOCK
            rem = S % BLOCK
            Lg = S - S % GBL
            ns = Lg // GBL
            scale = 1.0 / jnp.sqrt(jnp.asarray(d, q.dtype))
            k_str = k[:, :, :Lg].reshape(B, Hn, ns, GBL, d)[:, :, :, -1, :]
            v_str = v[:, :, :Lg].reshape(B, Hn, ns, GBL, d)[:, :, :, -1, :]
            outs = []
            if nb > 0:
                L = nb * BLOCK
                fq = q[:, :, :L].reshape(B, Hn, nb, BLOCK, d)
                fk_loc = k[:, :, :L].reshape(B, Hn, nb, BLOCK, d)
                fv_loc = v[:, :, :L].reshape(B, Hn, nb, BLOCK, d)
                mloc = M[..., :L, :L].reshape(1, 1, nb, BLOCK, nb, BLOCK)
                mloc = jnp.moveaxis(jnp.diagonal(mloc, axis1=2, axis2=4), -1, 2)
                mstr = M[..., :L, :Lg].reshape(1, 1, nb, BLOCK, ns, GBL)[..., -1]
                fmask = jnp.concatenate([mstr, mloc], axis=-1)
                fk = jnp.concatenate([jnp.broadcast_to(k_str[:, :, None], (B, Hn, nb, ns, d)), fk_loc], axis=-2)
                fv = jnp.concatenate([jnp.broadcast_to(v_str[:, :, None], (B, Hn, nb, ns, d)), fv_loc], axis=-2)
                w = jnp.einsum('bhnqd,bhnkd->bhnqk', fq, fk) * scale + fmask
                w = jax.nn.softmax(w, axis=-1)
                o1 = jnp.einsum('bhnqk,bhnkd->bhnqd', w, fv).reshape(B, Hn, L, d)
                outs.append(o1)
            if rem > 0:
                sq = q[:, :, -rem:]
                sk = jnp.concatenate([k_str, k[:, :, -rem:]], axis=2)
                sv = jnp.concatenate([v_str, v[:, :, -rem:]], axis=2)
                mstr2 = M[..., -rem:, :Lg].reshape(1, 1, rem, ns, GBL)[..., -1]
                smask = jnp.concatenate([mstr2, M[..., -rem:, -rem:]], axis=-1)
                w2 = jnp.einsum('bhqd,bhkd->bhqk', sq, sk) * scale + smask
                w2 = jax.nn.softmax(w2, axis=-1)
                o2 = jnp.einsum('bhqk,bhkd->bhqd', w2, sv)
                outs.append(o2)
            return jnp.concatenate(outs, axis=-2) if len(outs) > 1 else outs[0]
        key = jax.random.key(seed)
        ks = jax.random.split(key, 4)
        B, S = (4, 288)
        return {'hidden_states': jax.random.normal(ks[0], (B, S, E), dtype=jnp.float32), 'c_attn_w': jax.random.normal(ks[1], (E, 3 * E), dtype=jnp.float32) * 0.02, 'c_attn_b': jnp.zeros((3 * E,), dtype=jnp.float32), 'c_proj_w': jax.random.normal(ks[2], (E, E), dtype=jnp.float32) * 0.02, 'c_proj_b': jnp.zeros((E,), dtype=jnp.float32)}
    _L1_attn_in = _L1_attn_setup()

    def _L1_ffn_setup():
        import jax, jax.numpy as jnp
        import numpy as np
        B, N, D = (4, 256, 128)
        SPARSITY = 0.01
        key = jax.random.key(seed)
        k1, k2, k3 = jax.random.split(key, 3)
        x = jax.random.normal(k1, (B, N, D), dtype=jnp.float32)
        spatial = jax.random.normal(k2, (D, D), dtype=jnp.float32) * 0.02
        freq = jnp.fft.fft(spatial, axis=-1)
        k = int(D * SPARSITY)
        mag = jnp.abs(freq)
        kth = jax.lax.top_k(mag, k)[0][:, -1:]
        w_sparse = jnp.where(mag >= kth, freq, 0.0 + 0j)
        bias = jax.random.normal(k3, (D,), dtype=jnp.float32) * 0.01
        return {'x': x, 'w_freq_real': jnp.real(w_sparse).astype(jnp.float32), 'w_freq_imag': jnp.imag(w_sparse).astype(jnp.float32), 'bias': bias}
    _L1_ffn_in = _L1_ffn_setup()
    _d = {'L0_attn_x': _L0_attn_in['x'], 'L0_attn_WQ': _L0_attn_in['WQ'], 'L0_attn_WK': _L0_attn_in['WK'], 'L0_attn_WO': _L0_attn_in['WO'], 'L0_attn_Winv': _L0_attn_in['Winv'], 'L0_attn_U_b': _L0_attn_in['U_b'], 'L0_attn_V_b': _L0_attn_in['V_b'], 'L0_attn_W_b': _L0_attn_in['W_b'], 'L0_attn_bias_b': _L0_attn_in['bias_b'], 'L0_attn_U_t': _L0_attn_in['U_t'], 'L0_attn_V_t': _L0_attn_in['V_t'], 'L0_attn_W_t': _L0_attn_in['W_t'], 'L0_attn_X_t': _L0_attn_in['X_t'], 'L0_attn_bias_t': _L0_attn_in['bias_t'], 'L0_attn_alpha_bi': _L0_attn_in['alpha_bi'], 'L0_attn_alpha_tri': _L0_attn_in['alpha_tri'], 'L0_ffn_W1': _L0_ffn_in['W1'], 'L0_ffn_b1': _L0_ffn_in['b1'], 'L0_ffn_W2': _L0_ffn_in['W2'], 'L0_ffn_b2': _L0_ffn_in['b2'], 'L0_ffn_Wr': _L0_ffn_in['Wr'], 'L0_ffn_br': _L0_ffn_in['br'], 'L1_attn_c_attn_w': _L1_attn_in['c_attn_w'], 'L1_attn_c_attn_b': _L1_attn_in['c_attn_b'], 'L1_attn_c_proj_w': _L1_attn_in['c_proj_w'], 'L1_attn_c_proj_b': _L1_attn_in['c_proj_b'], 'L1_ffn_w_freq_real': _L1_ffn_in['w_freq_real'], 'L1_ffn_w_freq_imag': _L1_ffn_in['w_freq_imag'], 'L1_ffn_bias': _L1_ffn_in['bias']}
    _x0 = _d['L0_attn_x']
    _d['L0_attn_x'] = jax.random.normal(jax.random.fold_in(jax.random.key(seed), 1), (4, 1024, 128), dtype=_x0.dtype)
    del _x0
    return _d

def reference(L0_attn_x, L0_attn_WQ, L0_attn_WK, L0_attn_WO, L0_attn_Winv, L0_attn_U_b, L0_attn_V_b, L0_attn_W_b, L0_attn_bias_b, L0_attn_U_t, L0_attn_V_t, L0_attn_W_t, L0_attn_X_t, L0_attn_bias_t, L0_attn_alpha_bi, L0_attn_alpha_tri, L0_ffn_W1, L0_ffn_b1, L0_ffn_W2, L0_ffn_b2, L0_ffn_Wr, L0_ffn_br, L1_attn_c_attn_w, L1_attn_c_attn_b, L1_attn_c_proj_w, L1_attn_c_proj_b, L1_ffn_w_freq_real, L1_ffn_w_freq_imag, L1_ffn_bias):

    def _L0_attn_ref(x, WQ, WK, WO, Winv, U_b, V_b, W_b, bias_b, U_t, V_t, W_t, X_t, bias_t, alpha_bi, alpha_tri):
        import jax, jax.numpy as jnp
        import numpy as np
        B, T, D, R = (4, 256, 128, 64)
        Tlen = x.shape[1]
        Q = x @ WQ.T
        K = x @ WK.T
        invQ = Q @ Winv.T
        invK = K @ Winv.T
        counts = jnp.arange(1, Tlen + 1, dtype=x.dtype)[None, :, None]
        z = jnp.cumsum(x, axis=1) / counts
        fwd_r = Q @ V_b * jnp.cumsum(K @ W_b, axis=1)
        inv_r = jnp.cumsum(invK @ V_b, axis=1) * (invQ @ W_b)
        tri_r = Q @ V_t * jnp.cumsum(K @ W_t, axis=1) * (z @ X_t)
        sum_fwd = fwd_r @ U_b.T + counts * bias_b
        sum_inv = inv_r @ U_b.T + counts * bias_b
        sum_tri = tri_r @ U_t.T + counts * bias_t
        out = (sum_fwd + alpha_bi * sum_inv + alpha_tri * sum_tri) / counts
        return out @ WO.T

    def _L0_ffn_ref(x, W1, b1, W2, b2, Wr, br):
        import jax, jax.numpy as jnp
        import numpy as np
        D = 128
        H = 256
        E = 8
        K = 2
        B, T = (4, 256)
        Bb, Tt, Dd = x.shape
        xf = x.reshape(-1, Dd)
        logits = xf @ Wr + br
        topk_val, topk_idx = jax.lax.top_k(logits, K)
        scores = jax.nn.softmax(topk_val, axis=-1)
        h = jnp.einsum('nd,edh->enh', xf, W1) + b1[:, None, :]
        a, g = jnp.split(h, 2, axis=-1)
        act = jax.nn.silu(a) * g
        out_e = jnp.einsum('enh,ehd->end', act, W2) + b2[:, None, :]
        out_ne = out_e.transpose(1, 0, 2)
        gathered = jnp.take_along_axis(out_ne, topk_idx[:, :, None], axis=1)
        out = jnp.sum(gathered * scores[:, :, None], axis=1)
        return out.reshape(Bb, Tt, Dd)

    def _L1_attn_ref(hidden_states, c_attn_w, c_attn_b, c_proj_w, c_proj_b):
        import jax, jax.numpy as jnp
        import numpy as np
        BLOCK = 64
        NUM_GLOBAL = 16
        GBL = BLOCK // NUM_GLOBAL
        NEG = -10000.0
        E = 128
        H = 16

        def _sparse_attn(q, k, v, M):
            B, Hn, S, d = q.shape
            nb = S // BLOCK
            rem = S % BLOCK
            Lg = S - S % GBL
            ns = Lg // GBL
            scale = 1.0 / jnp.sqrt(jnp.asarray(d, q.dtype))
            k_str = k[:, :, :Lg].reshape(B, Hn, ns, GBL, d)[:, :, :, -1, :]
            v_str = v[:, :, :Lg].reshape(B, Hn, ns, GBL, d)[:, :, :, -1, :]
            outs = []
            if nb > 0:
                L = nb * BLOCK
                fq = q[:, :, :L].reshape(B, Hn, nb, BLOCK, d)
                fk_loc = k[:, :, :L].reshape(B, Hn, nb, BLOCK, d)
                fv_loc = v[:, :, :L].reshape(B, Hn, nb, BLOCK, d)
                mloc = M[..., :L, :L].reshape(1, 1, nb, BLOCK, nb, BLOCK)
                mloc = jnp.moveaxis(jnp.diagonal(mloc, axis1=2, axis2=4), -1, 2)
                mstr = M[..., :L, :Lg].reshape(1, 1, nb, BLOCK, ns, GBL)[..., -1]
                fmask = jnp.concatenate([mstr, mloc], axis=-1)
                fk = jnp.concatenate([jnp.broadcast_to(k_str[:, :, None], (B, Hn, nb, ns, d)), fk_loc], axis=-2)
                fv = jnp.concatenate([jnp.broadcast_to(v_str[:, :, None], (B, Hn, nb, ns, d)), fv_loc], axis=-2)
                w = jnp.einsum('bhnqd,bhnkd->bhnqk', fq, fk) * scale + fmask
                w = jax.nn.softmax(w, axis=-1)
                o1 = jnp.einsum('bhnqk,bhnkd->bhnqd', w, fv).reshape(B, Hn, L, d)
                outs.append(o1)
            if rem > 0:
                sq = q[:, :, -rem:]
                sk = jnp.concatenate([k_str, k[:, :, -rem:]], axis=2)
                sv = jnp.concatenate([v_str, v[:, :, -rem:]], axis=2)
                mstr2 = M[..., -rem:, :Lg].reshape(1, 1, rem, ns, GBL)[..., -1]
                smask = jnp.concatenate([mstr2, M[..., -rem:, -rem:]], axis=-1)
                w2 = jnp.einsum('bhqd,bhkd->bhqk', sq, sk) * scale + smask
                w2 = jax.nn.softmax(w2, axis=-1)
                o2 = jnp.einsum('bhqk,bhkd->bhqd', w2, sv)
                outs.append(o2)
            return jnp.concatenate(outs, axis=-2) if len(outs) > 1 else outs[0]
        B, S, Em = hidden_states.shape
        d = Em // H
        qkv = hidden_states @ c_attn_w + c_attn_b
        q, k, v = jnp.split(qkv, 3, axis=-1)

        def split_heads(t):
            return t.reshape(B, S, H, d).transpose(0, 2, 1, 3)
        q, k, v = (split_heads(q), split_heads(k), split_heads(v))
        causal = jnp.tril(jnp.ones((S, S), dtype=bool))
        M = jnp.where(causal, 0.0, NEG).astype(hidden_states.dtype)[None, None]
        attn_out = _sparse_attn(q, k, v, M)
        attn_out = attn_out.transpose(0, 2, 1, 3).reshape(B, S, Em)
        return attn_out @ c_proj_w + c_proj_b

    def _L1_ffn_ref(x, w_freq_real, w_freq_imag, bias):
        import jax, jax.numpy as jnp
        import numpy as np
        B, N, D = (4, 256, 128)
        SPARSITY = 0.01
        w = jax.lax.complex(w_freq_real, w_freq_imag)
        x_freq = jnp.fft.fft(x, axis=-1)
        y_freq = jnp.einsum('bnd,do->bno', x_freq, w)
        y = jnp.real(jnp.fft.ifft(y_freq, axis=-1))
        return y + bias
    x = L0_attn_x
    xn = _layernorm(x, axis=-1)
    x = x + _L0_attn_ref(xn, L0_attn_WQ, L0_attn_WK, L0_attn_WO, L0_attn_Winv, L0_attn_U_b, L0_attn_V_b, L0_attn_W_b, L0_attn_bias_b, L0_attn_U_t, L0_attn_V_t, L0_attn_W_t, L0_attn_X_t, L0_attn_bias_t, L0_attn_alpha_bi, L0_attn_alpha_tri) + _L0_ffn_ref(xn, L0_ffn_W1, L0_ffn_b1, L0_ffn_W2, L0_ffn_b2, L0_ffn_Wr, L0_ffn_br)
    xn = _layernorm(x, axis=-1)
    x = x + _L1_attn_ref(xn, L1_attn_c_attn_w, L1_attn_c_attn_b, L1_attn_c_proj_w, L1_attn_c_proj_b) + _L1_ffn_ref(xn, L1_ffn_w_freq_real, L1_ffn_w_freq_imag, L1_ffn_bias)
    return x

_drawn_inputs = setup_inputs


def setup_inputs(seed=0):
    import zlib

    import numpy as np

    out = dict(_drawn_inputs(seed))
    spreads = {'L0_attn_bias_b': (0.0, 2.0),
     'L0_attn_bias_t': (0.0, 2.0),
     'L0_ffn_b1': (0.0, 0.8),
     'L0_ffn_b2': (0.0, 2.0),
     'L0_ffn_br': (0.0, 0.1),
     'L1_attn_c_attn_b': (0.0, 2.0),
     'L1_attn_c_proj_b': (0.0, 2.0)}
    factors = {'L0_attn_WQ': 8.0,
     'L0_attn_WK': 8.0,
     'L0_attn_Winv': 8.0,
     'L0_attn_U_b': 8.0,
     'L0_attn_V_b': 8.0,
     'L0_attn_W_b': 8.0,
     'L0_attn_U_t': 45.268,
     'L0_attn_V_t': 39.902,
     'L0_attn_W_t': 42.999,
     'L0_attn_X_t': 35.919,
     'L0_ffn_W1': 8.0,
     'L0_ffn_W2': 8.0,
     'L1_attn_c_attn_w': 64.0,
     'L1_ffn_bias': 200.0,
     'L1_attn_c_proj_w': 6.908,
     'L1_ffn_w_freq_real': 8.0,
     'L1_ffn_w_freq_imag': 8.0}
    for name, (base, spread) in spreads.items():
        noise = np.random.default_rng([zlib.crc32(name.encode()), seed]).standard_normal(out[name].shape)
        drawn = base * np.exp(spread * noise) if base else spread * noise
        out[name] = jnp.asarray(drawn.astype(out[name].dtype))
    for name, factor in factors.items():
        out[name] = (out[name] * factor).astype(out[name].dtype)
    return out
```

```python
from contextlib import ExitStack

import numpy as np

import concourse.bass as bass
from concourse import mybir

F32 = mybir.dt.float32
F32R = mybir.dt.float32r
ALU = mybir.AluOpType
ACT = mybir.ActivationFunctionType
AX = mybir.AxisListType

B, T, D, R = 4, 1024, 128, 64
P = 128
NT = B * T // P
TB = T // P
C = 512
NC = B * T // C
E, HF = 8, 256
NH, HD = 16, 8
HG = 4
ST = 4
NS = T // ST
KW = NS + P
MASK = -10000.0
FAR = -1.0e38
EPS = 1e-5
KQ = 3 * HD
KM = KQ + 2

WEIGHTS = ["WQ", "WK", "WO", "Winv"]
THIN = ["U_b", "V_b", "W_b", "U_t", "V_t", "W_t", "X_t"]


class Chain:

    def __init__(self, eng, sem):
        self.eng, self.sem, self.n, self.turn, self.count = eng, sem, 0, None, 0

    def loop(self, turn, count):
        self.turn, self.count, self.at = turn, count, self.n

    def done(self, turns):
        assert self.n - self.at == self.count, (self.n - self.at, self.count)
        self.n, self.turn = self.at + turns * self.count, None

    def __call__(self, ins):
        self.n += 1
        ins.then_inc(self.sem, 1)
        self.eng.wait_ge(self.sem, self.n if self.turn is None else self.turn * self.count + self.n)


MISC = ("V", "K", "M", "D", "F")
MB = (2, 7)
N_LOADS = 30
PARTS = (2, 0, 1)


def value_slots(i):
    return [range(0, 3), range(3, 6), range(6, 8), range(8, 10)][i]


def batch_steps():
    steps = [("xT", 0, 0), ("xT", 0, 1)] + [("V", 0, i) for i in range(4)]
    steps += [("K", 0, i) for i in range(4)] + [("A", 0, i) for i in range(32)] + [("N", 0, 0), ("M", 0, 0)]
    for g in range(HG):
        done = 0
        for i in range(24):
            steps.append(("S", g, i))
            if i >= 2:
                steps.append(("P", g, i - 2))
            if i == 13:
                steps.append(("O", g, 0))
            if i == 16:
                steps.append(("D", g, 0))
            if i == 4 and g:
                steps.append(("D", g - 1, 1))
            if g < HG - 1:
                if i < 4:
                    steps.append(("K", g + 1, i))
                else:
                    upto = min(32, (i - 3) * 2)
                    steps += [("A", g + 1, j) for j in range(done, upto)]
                    done = upto
                if i == 21:
                    steps += [("N", g + 1, 0), ("M", g + 1, 0)]
        steps += [("P", g, 22), ("P", g, 23), ("O", g, 1)]
    return steps + [("D", HG - 1, 1), ("F", 0, 0), ("F", 0, 1)]


def build(nc, a, out):
    x_d = a["L0_attn_x"].rearrange("b (t p) d -> p (b t) d", p=P)
    out_d = out.rearrange("b (t p) d -> b p t d", p=P)
    with ExitStack() as ctx:
        def sb(name, shape, dt=F32):
            return ctx.enter_context(nc.sbuf_tensor(name, shape, dt))

        def sem(name):
            return ctx.enter_context(nc.semaphore(name))

        bank = [ctx.enter_context(nc.psum_tensor(f"bank{i}", [P, C], F32)) for i in range(8)]

        x = sb("x_tok", [P, NT, D])
        tokens_a = sb("tokens_a", [P, 2 * B * T])
        weights_a = sb("weights_a", [P, 3 * E * 2 * D])
        routing_a = sb("routing_a", [P, B * T])
        xnT = tokens_a[:, 0:B * T]
        z = tokens_a[:, B * T:2 * B * T]
        xst = sb("xst", [P, 2, 4, D])
        stats = sb("stats", [P, NT, 6])
        ln = sb("ln", [P, 10, NT])
        MEAN, RSTD = 0, 1
        ident = sb("ident", [P, P])
        identr = sb("identr", [P, P], F32R)
        ones = sb("ones", [P, T])
        rcount = sb("rcount", [P, T])
        w = {n: sb("w_" + n, [P, D]) for n in WEIGHTS}
        vb_t = sb("rq", [P, 3 * R])
        wb_t = sb("rk", [P, 3 * R])
        ub2 = sb("ub2", [P, 2 * R])
        ut = sb("ut", [P, R])
        LQ = sb("LQ", [P, 3 * R])
        LK = sb("LK", [P, 4 * R])
        UB = sb("UB", [P, D])
        UT = sb("UT", [R, D])
        woT = sb("woT", [P, D])
        al = sb("al", [P, 4])
        bb = sb("bb", [P, 4])
        dft = sb("dft", [P, 3, D])
        wf = sb("wf", [P, 2, D])
        aT = sb("aT", [P, 2, D])
        G = sb("G", [P, D])
        W1 = weights_a[:, 0:E * 2 * HF].rearrange("p (e h) -> p e h", e=E)
        b1 = sb("b1", [P, 2 * HF // P, E])
        W2 = weights_a[:, E * 2 * HF:E * 3 * HF].rearrange("p (e k d) -> p e k d", e=E, k=2)
        b2a = sb("b2a", [E + 1, D])
        Wr = sb("Wr", [P, E])
        brb = sb("brb", [P, E])
        lg = sb("lg", [P, NT, E])
        gt = sb("gt", [P, 4, NT, E])
        gs = sb("gs", [P, 4, NT])
        desc = sb("desc", [P, E])
        w9 = sb("w9", [P, NT, E + 1])
        w9T = routing_a[0:E + 1, :]
        w9c = sb("w9c", [E + 1, C])
        sa = sb("sa", [P, C])
        sB = sb("sB", [P, C])
        sc = sb("sc", [R, C])
        tc = sb("tc", [R, C])
        tri = sb("tri", [R, C])
        sil = sb("sil", [P, 2, C])
        actT = sb("actT", [P, 2, 2, C])
        yw = sb("yw", [P, 2, 4, D])
        cw = sb("cw", [P, 3 * D])
        cb = sb("cb", [1, 3 * D])
        wrep = sb("wrep", [P, 2, NH, 32])
        brep = sb("brep", [1, 2, NH, 32])
        bqk = sb("bqk", [P, 2, HG])
        bqm = sb("bqm", [P, 2, HG])
        lowm = sb("lowm", [P, 2])
        bvb = sb("bvb", [P, D])
        cp = sb("cp", [P, HG, D])
        bsel = sb("bsel", [P, P])
        mask1 = routing_a[:, 0:TB * KW].rearrange("p (t k) -> p t k", t=TB)
        mstr = sb("mstr", [P, C])
        mloc = sb("mloc", [P, P])
        mstr_r = sb("mstr_r", [P, C], F32R)
        mloc_r = sb("mloc_r", [P, P], F32R)
        maskc = sb("maskc", [P, 2])
        xn2T = sb("xn2T", [P, T])
        NV = (2 + TB) * NH * 32
        vaug = tokens_a[:, 0:NV].rearrange("p (j h e) -> p j h e", h=NH, e=32)
        hi = sb("hi", [P, 2, C], F32R)
        qs = sb("qs", [P, 2, T], F32R)
        ks = sb("ks", [P, 2, T], F32R)
        junk = routing_a[:, TB * KW:(TB + 2) * KW].rearrange("p (t k) -> p t k", t=2)
        mx = sb("mx", [P, 2, 4, TB])
        nm = sb("nm", [P, 4, 2, TB])
        nmr = sb("nmr", [P, 4, TB], F32R)
        mT = sb("mT", [TB * 8, P], F32R)
        pT = tokens_a[:, NV:NV + 4 * C].rearrange("p (u q) -> p u q", u=4)
        onum = tokens_a[:, NV + 4 * C:NV + 6 * C].rearrange("p (u q) -> p u q", u=2)
        oT = weights_a[:, 0:HG * T].rearrange("p (g q) -> p g q", g=HG)
        rden = weights_a[:, HG * T:HG * T + 2 * C].rearrange("p (u q) -> p u q", u=2)
        yo = weights_a[:, HG * T + 2 * C:HG * T + 4 * C].rearrange("p (u t d) -> p u t d", u=2, t=4)


        x_in = [sem(f"x_in{b}") for b in range(B)]
        w_in, w1_in, cp_in = sem("w_in"), sem("w1_in"), sem("cp_in")
        g_const = sem("g_const")
        g_chain, d_chain = sem("g_chain"), sem("d_chain")
        var_ready, sq_ready = sem("var_ready"), sem("sq_ready")
        xn_ready, xT_done, xT_used = sem("xn_ready"), sem("xT_done"), sem("xT_used")
        z_sum, z_ready = sem("z_sum"), sem("z_ready")
        set1, set1_sb, set2, set2_sb = sem("set1"), sem("set1_sb"), sem("set2"), sem("set2_sb")
        identr_ready = sem("identr_ready")
        lg_ps, dif_ready, exp_ready, w9_ready = sem("lg_ps"), sem("dif_ready"), sem("exp_ready"), sem("w9_ready")
        w9_ps, w9T_ready = sem("w9_ps"), sem("w9T_ready")
        r_ps, r_act, r_dve = sem("r_ps"), sem("r_act"), sem("r_dve")
        h_ps, sil_ready, h_used = sem("h_ps"), sem("sil_ready"), sem("h_used")
        y_ps, y_used, yw_used = sem("y_ps"), sem("y_used"), sem("yw_used")
        w9c_ready = sem("w9c_ready")
        m_ps, m_used = sem("m_ps"), [sem("m_used0"), sem("m_used1")]
        hi_ready, hi_used = sem("hi_ready"), sem("hi_used")
        a_ps, a_used = sem("a_ps"), sem("a_used")
        n_part, n_ready, m_rows = sem("n_part"), sem("n_ready"), sem("m_rows")
        s_ps, p_ready, p_used = sem("s_ps"), sem("p_ready"), sem("p_used")
        o_ps, on_ready, oT_ready = sem("o_ps"), sem("on_ready"), sem("oT_ready")
        apart = sem("apart")
        out_done = [sem(f"out_done{i}") for i in range(2)]

        block = ctx.enter_context(nc.Block())

        steps = batch_steps()
        misc_at = {s: n for n, s in enumerate(s for s in steps if s[0] in MISC)}
        n_of = {k: sum(s[0] == k for s in steps) for k in {s[0] for s in steps}}
        n_misc = len(misc_at)
        assert n_misc % 2 == 0

        def misc_full(eng, b, step):
            eng.wait_ge(m_ps, b * n_misc + misc_at[step] + 1)

        def misc_read(eng, b, step):
            eng.wait_ge(m_used[misc_at[step] % 2], b * (n_misc // 2) + misc_at[step] // 2 + 2)

        def misc_bank(step):
            return bank[MB[misc_at[step] % 2]]

        @block.sync
        def _(sp):
            for b in range(B):
                sp.dma_start(x[:, b * TB:(b + 1) * TB, :], x_d[:, b * TB:(b + 1) * TB, :]).then_inc(x_in[b], 16)
            sp.dma_start(W1[:, :, :], a["L0_ffn_W1"].rearrange("e d h -> d e h")).then_inc(w1_in, 16)
            for k in range(2):
                sp.dma_start(W2[:, :, k, :], a["L0_ffn_W2"][:, k * P:(k + 1) * P, :].rearrange("e p d -> p e d")).then_inc(w1_in, 16)
            sp.dma_start(b1[:, :, :], a["L0_ffn_b1"]).then_inc(w1_in, 16)
            with sp.Fori(0, B) as b:
                for g in range(HG):
                    misc_read(sp, b, ("M", g, 0))
                    for r in range(4):
                        for s in range(2):
                            row = r * 2 * TB + s * TB
                            sp.dma_start(qs[32 * r + KQ + s:32 * r + KQ + s + 1, g % 2, :].bitcast(F32),
                                         mT[row:row + TB, :].bitcast(F32)).then_inc(m_rows, 16)
                for k in range(2):
                    misc_read(sp, b, ("F", 0, k))
                    sp.dma_start(out_d[bass.ds(b, 1), :, 4 * k:4 * k + 4, :].rearrange("a p t d -> (a p) t d"),
                                 yo[:, k, :, :]).then_inc(out_done[k], 16)
            for k in range(2):
                sp.wait_ge(out_done[k], 16 * (B + 1))

        @block.scalar
        def _(act):
            act.sem_inc(r_act, 2)
            act.sem_inc(xT_used, 2)
            act.sem_inc(out_done[0], 16)
            act.sem_inc(out_done[1], 16)
            act.sem_inc(p_ready, 3)
            act.sem_inc(on_ready, 1)
            loads = [(w[k][:, :], a["L0_attn_" + k]) for k in WEIGHTS]
            loads += [(vb_t[:, 0:R], a["L0_attn_V_b"]), (vb_t[:, 2 * R:3 * R], a["L0_attn_V_t"]),
                      (wb_t[:, 0:R], a["L0_attn_W_b"]), (wb_t[:, 2 * R:3 * R], a["L0_attn_W_t"]),
                      (ub2[:, 0:R], a["L0_attn_U_b"]), (ub2[:, R:2 * R], a["L0_attn_U_b"]),
                      (ut[:, :], a["L0_attn_U_t"]), (LK[:, 3 * R:4 * R], a["L0_attn_X_t"]),
                      (al[:, 0:1], a["L0_attn_alpha_bi"].partition_broadcast(P)),
                      (al[:, 1:2], a["L0_attn_alpha_tri"].partition_broadcast(P)),
                      (bb[:, 0:1], a["L0_attn_bias_b"].rearrange("(p a) -> p a", a=1)),
                      (bb[:, 1:2], a["L0_attn_bias_t"].rearrange("(p a) -> p a", a=1)),
                      (dft[:, :, :], a["dft"]), (wf[:, 0, :], a["L1_ffn_w_freq_real"]),
                      (wf[:, 1, :], a["L1_ffn_w_freq_imag"]), (b2a[1:E + 1, :], a["L0_ffn_b2"]),
                      (Wr[:, :], a["L0_ffn_Wr"]), (brb[:, :], a["L0_ffn_br"].partition_broadcast(P)),
                      (cw[:, :], a["L1_attn_c_attn_w"]),
                      (cb[:, :], a["L1_attn_c_attn_b"].rearrange("(a n) -> a n", a=1)),
                      (bvb[:, :], a["L1_attn_c_attn_b"][2 * D:3 * D].partition_broadcast(P)),
                      (lowm[:, :], a["low_rows"]), (rcount[:, :], a["rcount"].partition_broadcast(P)),
                      (desc[:, :], a["desc"].partition_broadcast(P)), (ident[:, :], a["ident"]),
                      (bsel[:, :], a["bsel"])]
            assert len(loads) == N_LOADS
            for dst, src in loads:
                act.dma_start(dst, src).then_inc(w_in, 16)
            act.wait_ge(g_const, 1)
            for r in range(4):
                act.dma_start(cp[32 * r:32 * r + HD, :, :],
                              a["L1_attn_c_proj_w"].rearrange("(g r e) n -> r e g n", g=HG, r=4)[r]).then_inc(cp_in, 16)
            act.dma_start(cp[HD:HD + 1, 0, :], a["L1_attn_c_proj_b"].rearrange("(a n) -> a n", a=1)).then_inc(cp_in, 16)
            act.dma_start(cp[32 + HD:33 + HD, 0, :], a["L1_ffn_bias"].rearrange("(a n) -> a n", a=1)).then_inc(cp_in, 16)

            def root(n):
                act.wait_ge(var_ready, n)
                nc.scalar.activation(ln[:, 2, :], ln[:, 1, :], ACT.Sqrt).then_inc(sq_ready, 1)

            def xT_out(dst, turn, g):
                act.wait_ge(xT_done, turn * 2 + g + 3)
                nc.scalar.activation(dst, bank[g][:, :], ACT.Copy).then_inc(xT_used, 1)

            root(1)
            with act.Fori(0, NC // 2) as i:
                for g in range(2):
                    xT_out(xnT[:, bass.ds(i * 2 * C + g * C, C)], i, g)
            act.wait_ge(w_in, 16 * N_LOADS)
            nc.scalar.activation(identr[:, :], ident[:, :], ACT.Copy).then_inc(identr_ready, 1)
            act.wait_ge(g_const, 2)
            nc.scalar.activation(mstr_r[:, :], mstr[:, :], ACT.Copy).then_inc(identr_ready, 1)
            nc.scalar.activation(mloc_r[:, :], mloc[:, :], ACT.Copy).then_inc(identr_ready, 1)
            act.wait_ge(dif_ready, 1)
            nc.scalar.activation(gs[:, 3, :], gs[:, 2, :], ACT.Exp).then_inc(exp_ready, 1)
            for k in range(NC):
                act.wait_ge(w9_ps, k + 1)
                nc.scalar.activation(w9T[:, k * C:(k + 1) * C], bank[k % 4][0:E + 1, :], ACT.Copy).then_inc(w9T_ready, 1)

            act.wait_ge(w1_in, 16 * 4)
            with act.Fori(0, NC) as c:
                act.wait_ge(r_ps, c * 5 + 1)
                act.wait_ge(r_dve, c * 4 + 1)
                nc.scalar.activation(sa[:, :], bank[6][:, :], ACT.Copy).then_inc(r_act, 1)
                act.wait_ge(r_ps, c * 5 + 3)
                act.wait_ge(r_dve, c * 4 + 2)
                nc.scalar.activation(sc[:, :], bank[6][0:R, :], ACT.Copy).then_inc(r_act, 1)
                for e in range(E):
                    for j in range(2):
                        u = 2 * e + j
                        act.wait_ge(h_ps, c * 2 * E + u + 1)
                        act.wait_ge(h_used, c * 2 * E + u + 1)
                        nc.scalar.activation(sil[:, u % 2, :], bank[2 * (u % 2)][:, :], ACT.Silu,
                                             bias=b1[:, j, e:e + 1]).then_inc(sil_ready, 1)

            root(2)
            with act.Fori(0, B) as b:
                n = dict.fromkeys(n_of, 0)
                for step in steps:
                    kind, g, i = step
                    if kind == "xT":
                        xT_out(xn2T[:, i * C:(i + 1) * C], b + NC // 2, i)
                    elif kind == "K":
                        misc_full(act, b, step)
                        act.wait_ge(hi_used, b * n_of["K"] + n["K"] + 1)
                        nc.scalar.activation(hi[:, n["K"] % 2, :], misc_bank(step)[:, :], ACT.Identity,
                                             bias=bqm[:, i // 2, g:g + 1],
                                             scale=lowm[:, i // 2:i // 2 + 1]).then_inc(hi_ready, 1)
                    elif kind == "M":
                        misc_full(act, b, step)
                        act.wait_ge(m_rows, (b * HG + g) * 128 + 128)
                        nc.scalar.activation(mT[:, :], misc_bank(step)[0:8 * TB, 0:P],
                                             ACT.Copy).then_inc(m_used[misc_at[step] % 2], 1)
                    elif kind == "S":
                        u = n["S"]
                        part, qc = PARTS[i % 3], i // 12
                        act.wait_ge(s_ps, b * n_of["S"] + u + 1)
                        act.wait_ge(p_used, b * n_of["S"] + u + 1)
                        nc.scalar.activation(pT[:, u % 4, :], bank[3 + u % 3][:, :], ACT.Exp,
                                             bias=maskc[:, 0:1] if (part, qc) == (1, 0) else 0.0).then_inc(p_ready, 1)
                    elif kind == "O":
                        act.wait_ge(o_ps, b * n_of["O"] + n["O"] + 1)
                        act.wait_ge(oT_ready, b * n_of["O"] + n["O"] + 1)
                        nc.scalar.activation(onum[:, i, :], bank[6][:, :], ACT.Copy).then_inc(on_ready, 1)
                    n[kind] += 1

        @block.gpsimd
        def _(pool):
            pool.sem_inc(yw_used, 2)
            pool.sem_inc(oT_ready, 2)
            pool.sem_inc(m_rows, 128)
            link = Chain(pool, g_chain)
            nc.gpsimd.memset(ones[:, :], 1.0)
            link(nc.gpsimd.memset(cp[:, :, :], 0.0))
            pool.sem_inc(g_const, 1)
            nc.gpsimd.memset(maskc[:, :], MASK)
            nc.gpsimd.memset(w9[:, :, 0:1], 1.0)
            nc.gpsimd.memset(mstr[:, :], 0.0)
            link(nc.gpsimd.memset(mloc[:, :], 0.0))
            nc.gpsimd.memset(wrep[:, :, :, :], 0.0)
            nc.gpsimd.memset(brep[:, :, :, :], 0.0)
            nc.gpsimd.affine_select(out=mstr[:, :], in_=mstr[:, :], compare_op=ALU.is_ge, fill=MASK,
                                    base=-(ST - 1), pattern=[[1, C]], channel_multiplier=-ST)
            link(nc.gpsimd.affine_select(out=mloc[:, :], in_=mloc[:, :], compare_op=ALU.is_ge, fill=MASK,
                                         base=0, pattern=[[1, P]], channel_multiplier=-1))
            for lo, other in ((0, 64), (64, 0)):
                last = nc.gpsimd.memset(mloc[lo:lo + 64, other:other + 64], FAR)
            link(last)
            link(nc.gpsimd.memset(brep[:, 1, :, KQ:KM], 1.0))
            pool.sem_inc(g_const, 1)
            pool.wait_ge(w_in, 16 * N_LOADS)
            scale = float(np.float32(1) / np.sqrt(np.float32(HD)))
            for src, dst in ((cw, wrep), (cb, brep)):
                for s in range(3):
                    for k in range(2):
                        last = nc.gpsimd.tensor_scalar(dst[:, k, :, s * HD:(s + 1) * HD],
                                                       src[:, k * D:(k + 1) * D].rearrange("p (h e) -> p h e", h=NH),
                                                       scale if k == 0 else 1.0, None, ALU.mult)
            last.then_inc(g_const, 1)
            for b in range(B):
                pool.wait_ge(z_sum, b + 1)
                nc.gpsimd.tensor_tensor(z[:, b * T:(b + 1) * T], z[:, b * T:(b + 1) * T], rcount[:, :],
                                        ALU.mult).then_inc(z_ready, 1)
            pool.wait_ge(w9T_ready, NC)
            with pool.Fori(0, NC) as c:
                pool.wait_ge(r_dve, c * 4 + 4)
                nc.gpsimd.tensor_copy(w9c[:, :], w9T[:, bass.ds(c * C, C)]).then_inc(w9c_ready, 1)
                pool.wait_ge(r_dve, c * 4 + 8)
                for e in range(E):
                    pool.wait_ge(y_used, c * E + e + 3)
                    pool.wait_ge(yw_used, c * E + e + 2)
                    pool.sem_inc(apart, 1)
                    xs = x[:, bass.ds(c * 4, 4), :]
                    nc.gpsimd.tensor_tensor(xs, xs, yw[:, e % 2, :, :], ALU.add).then_inc(yw_used, 1)
            nc.gpsimd.memset(mask1, 0.0)
            link(nc.gpsimd.memset(vaug, 0.0))
            nc.gpsimd.memset(vaug[:, :, :, HD:HD + 1], 1.0)
            nc.gpsimd.affine_select(out=mask1[:, :, 0:NS], in_=mask1[:, :, 0:NS], compare_op=ALU.is_ge, fill=MASK,
                                    base=-(ST - 1), pattern=[[P, TB], [-ST, NS]], channel_multiplier=1)
            last = nc.gpsimd.affine_select(out=mask1[:, :, NS:KW], in_=mask1[:, :, NS:KW], compare_op=ALU.is_ge, fill=MASK,
                                           base=0, pattern=[[0, TB], [-1, P]], channel_multiplier=1)
            link(last)
            for lo, other in ((0, 64), (64, 0)):
                last = nc.gpsimd.memset(mask1[lo:lo + 64, :, NS + other:NS + other + 64], FAR)
            last.then_inc(g_const, 1)
            with pool.Fori(0, B) as b:
                for step in steps:
                    kind, g, i = step
                    if kind == "D":
                        misc_read(pool, b, step)
                        nc.gpsimd.tensor_tensor(oT[:, g, i * C:(i + 1) * C], onum[:, i, :], rden[:, i, :],
                                                ALU.mult).then_inc(oT_ready, 1)

        @block.vector
        def _(dve):
            dve.sem_inc(r_dve, 4)
            dve.sem_inc(h_used, 2)
            dve.sem_inc(y_used, 2)
            dve.sem_inc(a_used, 2)
            dve.sem_inc(m_used[0], 1)
            dve.sem_inc(m_used[1], 1)
            dve.sem_inc(hi_used, 2)
            link = Chain(dve, d_chain)
            V = nc.vector

            def layer_norm(turn):
                even, odd = stats[:, :, 1], stats[:, :, 4]
                mean, var, sd, s0, s1, rstd = (ln[:, k, :] for k in (0, 1, 2, 3, 4, 5))
                V.tensor_tensor(s0, even, odd, ALU.add)
                V.tensor_tensor(s1, even, odd, ALU.subtract)
                link(V.tensor_tensor(var, stats[:, :, 2], stats[:, :, 5], ALU.add))
                V.tensor_scalar(mean, s0, 0.5, None, ALU.mult)
                V.tensor_scalar(var, var, 1.0 / D, EPS, ALU.mult, ALU.add)
                link(V.tensor_tensor(s1, s1, s1, ALU.mult))
                V.scalar_tensor_tensor(out=var, in0=s1, scalar=0.25, in1=var, op0=ALU.mult, op1=ALU.add).then_inc(var_ready, 1)
                dve.wait_ge(sq_ready, turn)
                link(V.reciprocal(rstd, sd))
                link(V.tensor_tensor(s0, rstd, rstd, ALU.mult))
                link(V.tensor_tensor(s0, s0, var, ALU.mult))
                link(V.tensor_scalar(s0, s0, -0.5, 1.5, ALU.mult, ALU.add))
                link(V.tensor_tensor(rstd, rstd, s0, ALU.mult))

            def normalise(turn, tile, g):
                dve.wait_ge(xT_done, turn * 2 + g + 1)
                for t in range(4):
                    last = V.tensor_scalar(xst[:, g, t, :], x[:, tile(4 * g + t), :].rearrange("p a d -> p (a d)"),
                                           ln[:, 0, tile(4 * g + t)], ln[:, 5, tile(4 * g + t)],
                                           ALU.subtract, ALU.mult)
                last.then_inc(xn_ready, 1)

            for b in range(B):
                dve.wait_ge(x_in[b], 16)
                with dve.Fori(0, TB) as t:
                    V.bn_stats(stats[:, bass.ds(t + b * TB, 1), :].rearrange("p a s -> p (a s)"),
                               x[:, bass.ds(t + b * TB, 1), :].rearrange("p a d -> p (a d)"))
            link(V.memset(al[:, 2:3], 1.0))
            layer_norm(1)
            with dve.Fori(0, NC // 2) as i:
                for g in range(2):
                    normalise(i, lambda t: bass.ds(i * 8 + t, 1), g)

            dve.wait_ge(set1, 1)
            V.tensor_copy(vb_t[:, R:2 * R], bank[2][:, 0:R])
            V.tensor_copy(wb_t[:, R:2 * R], bank[2][:, R:2 * R])
            V.tensor_copy(woT[:, :], bank[2][:, 2 * R:2 * R + D])
            V.tensor_scalar(aT[:, :, :], bank[3][:, 0:2 * D].rearrange("p (k n) -> p k n", k=2), 1.0 / D, None, ALU.mult)
            V.tensor_copy(al[R:2 * R, 2:3], al[R:2 * R, 0:1])
            link(V.scalar_tensor_tensor(out=bb[:, 2:3], in0=bb[:, 0:1], scalar=al[:, 0:1], in1=bb[:, 0:1],
                                        op0=ALU.mult, op1=ALU.add))
            V.scalar_tensor_tensor(out=bb[:, 3:4], in0=bb[:, 1:2], scalar=al[:, 1:2], in1=bb[:, 2:3],
                                   op0=ALU.mult, op1=ALU.add).then_inc(set1_sb, 1)
            dve.wait_ge(g_const, 2)
            dve.wait_ge(xT_used, NC + 2)
            for b in range(B):
                V.tensor_tensor_scan(z[:, b * T:(b + 1) * T], ones[:, :], xnT[:, b * T:(b + 1) * T], 0.0,
                                     ALU.mult, ALU.add).then_inc(z_sum, 1)
            dve.wait_ge(set2, 1)
            V.tensor_copy(LQ[:, :], bank[4][:, 0:3 * R])
            V.tensor_copy(LK[:, 0:3 * R], bank[4][:, 3 * R:6 * R])
            V.tensor_copy(G[:, :], bank[4][:, 6 * R:8 * R])
            V.tensor_scalar(UB[:, :], bank[5][:, 0:D], al[:, 2:3], None, ALU.mult)
            V.tensor_scalar(UT[:, :], bank[5][0:R, D:2 * D], al[0:R, 1:2], None, ALU.mult)
            V.tensor_copy(b2a[0:1, :], bank[5][0:1, 2 * D:3 * D])
            link(V.tensor_copy(bqk[:, :, :], bank[5][:, 3 * D:3 * D + 8].rearrange("p (k g) -> p k g", k=2)))
            for k in range(2):
                last = V.tensor_scalar(bqm[:, k, :], bqk[:, k, :], lowm[:, k:k + 1], None, ALU.mult)
            last.then_inc(set2_sb, 1)

            dve.wait_ge(lg_ps, 1)
            wide = [P, NT, E]
            link(V.tensor_tensor(lg[:, :, :], bank[0][:, 0:NT * E].rearrange("p (t e) -> p t e", t=NT),
                                 brb[:, :].unsqueeze(1).broadcast_to(wide), ALU.add))

            def top(logits, hot, best, tmp):
                link(V.tensor_reduce(best, logits, AX.X, ALU.max))
                link(V.tensor_tensor(hot, logits, best.unsqueeze(2).broadcast_to(wide), ALU.is_equal))
                link(V.tensor_tensor(hot, hot, desc[:, :].unsqueeze(1).broadcast_to(wide), ALU.mult))
                link(V.tensor_reduce(tmp, hot, AX.X, ALU.max))
                link(V.tensor_tensor(hot, hot, tmp.unsqueeze(2).broadcast_to(wide), ALU.is_equal))

            top(lg[:, :, :], gt[:, 0, :, :], gs[:, 0, :], gs[:, 3, :])
            link(V.scalar_tensor_tensor(out=gt[:, 1, :, :], in0=gt[:, 0, :, :], scalar=-3.0e38, in1=lg[:, :, :],
                                        op0=ALU.mult, op1=ALU.add))
            top(gt[:, 1, :, :], gt[:, 2, :, :], gs[:, 1, :], gs[:, 3, :])
            V.tensor_tensor(gs[:, 2, :], gs[:, 1, :], gs[:, 0, :], ALU.subtract).then_inc(dif_ready, 1)
            dve.wait_ge(exp_ready, 1)
            link(V.tensor_scalar(gs[:, 0, :], gs[:, 3, :], 1.0, None, ALU.add))
            link(V.reciprocal(gs[:, 1, :], gs[:, 0, :]))
            link(V.tensor_tensor(gs[:, 2, :], gs[:, 3, :], gs[:, 1, :], ALU.mult))
            V.tensor_tensor(gt[:, 0, :, :], gt[:, 0, :, :], gs[:, 1, :].unsqueeze(2).broadcast_to(wide), ALU.mult)
            link(V.tensor_tensor(gt[:, 2, :, :], gt[:, 2, :, :], gs[:, 2, :].unsqueeze(2).broadcast_to(wide), ALU.mult))
            V.tensor_tensor(w9[:, :, 1:E + 1], gt[:, 0, :, :], gt[:, 2, :, :], ALU.add).then_inc(w9_ready, 1)

            with dve.Fori(0, NC) as c:
                xs = x[:, bass.ds(c * 4, 4), :]

                def weigh(e):
                    dve.wait_ge(y_ps, c * E + e + 1)
                    dve.wait_ge(yw_used, c * E + e + 1)
                    V.tensor_tensor(yw[:, e % 2, :, :], bank[4 + e % 2][:, :].rearrange("p (t d) -> p t d", t=4),
                                    w9[:, bass.ds(c * 4, 4), e + 1:e + 2].broadcast_to([P, 4, D]),
                                    ALU.mult).then_inc(y_used, 1)

                dve.wait_ge(r_ps, c * 5 + 2)
                dve.wait_ge(r_act, c * 2 + 3)
                V.tensor_tensor(sB[:, :], sa[:, :], bank[7][:, :], ALU.mult).then_inc(r_dve, 1)
                dve.wait_ge(r_ps, c * 5 + 4)
                dve.wait_ge(r_act, c * 2 + 4)
                V.tensor_tensor(tc[:, :], sc[:, :], bank[7][0:R, :], ALU.mult).then_inc(r_dve, 1)
                dve.wait_ge(r_dve, c * 4 + 6)
                V.tensor_tensor(tri[:, :], tc[:, :], bank[7][R:2 * R, :], ALU.mult).then_inc(r_dve, 1)
                for e in range(E):
                    for j in range(2):
                        u = 2 * e + j
                        dve.wait_ge(sil_ready, c * 2 * E + u + 1)
                        V.scalar_tensor_tensor(out=actT[:, e % 2, j, :], in0=bank[2 * (u % 2) + 1][:, :],
                                               scalar=b1[:, 2 + j, e:e + 1], in1=sil[:, u % 2, :],
                                               op0=ALU.add, op1=ALU.mult).then_inc(h_used, 1)
                    if e == 0:
                        dve.wait_ge(r_ps, c * 5 + 5)
                        V.tensor_tensor(xs, xs, bank[7][:, :].rearrange("p (t d) -> p t d", t=4),
                                        ALU.add).then_inc(r_dve, 1)
                    else:
                        weigh(e - 1)
                weigh(E - 1)

            dve.wait_ge(yw_used, NC * E + 2)
            with dve.Fori(0, NT) as t:
                V.bn_stats(stats[:, bass.ds(t, 1), :].rearrange("p a s -> p (a s)"),
                           x[:, bass.ds(t, 1), :].rearrange("p a d -> p (a d)"))
            link(V.memset(al[:, 3:4], 1.0))
            layer_norm(2)
            dve.wait_ge(g_const, 4)
            with dve.Fori(0, B) as b:
                n = dict.fromkeys(n_of, 0)
                for step in steps:
                    kind, g, i = step
                    if kind == "xT":
                        normalise(b + NC // 2, lambda t: bass.ds(b * TB + t, 1), i)
                    elif kind == "V":
                        js = value_slots(i)
                        misc_full(dve, b, step)
                        V.tensor_tensor(vaug[:, js[0]:js[-1] + 1, :, 0:HD],
                                        misc_bank(step)[:, 0:len(js) * D].rearrange("p (j h e) -> p j h e", h=NH, e=HD),
                                        bvb[:, :].rearrange("p (h e) -> p h e", h=NH).unsqueeze(1)
                                        .broadcast_to([P, len(js), NH, HD]),
                                        ALU.add).then_inc(m_used[misc_at[step] % 2], 1)
                    elif kind == "K":
                        dve.wait_ge(hi_ready, b * n_of["K"] + n["K"] + 1)
                        dst = (qs, ks)[i // 2]
                        V.scalar_tensor_tensor(out=dst[:, g % 2, (i % 2) * C:(i % 2 + 1) * C], in0=misc_bank(step)[:, :],
                                               scalar=bqk[:, i // 2, g:g + 1], in1=hi[:, n["K"] % 2, :].bitcast(F32),
                                               op0=ALU.add, op1=ALU.subtract).then_inc(m_used[misc_at[step] % 2], 1)
                        misc_read(dve, b, step)
                        dve.sem_inc(hi_used, 1)
                    elif kind == "A":
                        u = n["A"]
                        t, r = divmod(i, 4)
                        dve.wait_ge(a_ps, b * n_of["A"] + u + 1)
                        dve.sem_inc(apart, 1)
                        V.tensor_tensor_reduce(junk[:, u % 2, :], bank[u % 2][:, 0:KW], mask1[:, t, :], 1.0, -3.0e38,
                                               ALU.add, ALU.max, mx[:, g % 2, r, t:t + 1]).then_inc(a_used, 1)
                    elif kind == "N":
                        dve.wait_ge(a_used, b * n_of["A"] + n["A"] + 2)
                        V.tensor_scalar(nmr[:, :, :], mx[:, g % 2, :, :], -1.0, None, ALU.mult).then_inc(n_part, 1)
                        dve.wait_ge(n_part, b * HG + g + 1)
                        V.tensor_copy(nm[:, :, 0, :], nmr[:, :, :].bitcast(F32))
                        V.scalar_tensor_tensor(out=nm[:, :, 1, :], in0=mx[:, g % 2, :, :], scalar=-1.0,
                                               in1=nmr[:, :, :].bitcast(F32), op0=ALU.mult,
                                               op1=ALU.subtract).then_inc(n_ready, 1)
                    elif kind == "D":
                        misc_full(dve, b, step)
                        V.reciprocal(rden[:, i, :], misc_bank(step)[:, :]).then_inc(m_used[misc_at[step] % 2], 1)
                    elif kind == "F":
                        misc_full(dve, b, step)
                        dve.wait_ge(out_done[i], b * 16 + 16)
                        V.tensor_tensor(yo[:, i, :, :], x[:, bass.ds(b * TB + 4 * i, 4), :],
                                        misc_bank(step)[:, :].rearrange("p (t d) -> p t d", t=4),
                                        ALU.add).then_inc(m_used[misc_at[step] % 2], 1)
                    n[kind] += 1

        @block.tensor
        def _(pe):
            pe.sem_inc(xT_done, 2)
            pe.sem_inc(p_used, 4)

            def transposes(turn, g):
                pe.wait_ge(xn_ready, turn * 2 + g + 1)
                pe.wait_ge(xT_used, turn * 2 + g + 1)
                for t in range(4):
                    last = pe.transpose(bank[g][:, t * P:(t + 1) * P], xst[:, g, t, :], ident[:, :])
                last.then_inc(xT_done, 1)

            def mm(o, l, r_, first=True, last=True, **k):
                return pe.matmul(o, l, r_, start=first, stop=last, **k)

            pe.wait_ge(w_in, 16 * N_LOADS)
            cos, sin, nsin = (dft[:, k, :] for k in range(3))
            mm(bank[2][:, 0:R], w["Winv"][:, :], wb_t[:, 0:R])
            mm(bank[2][:, R:2 * R], w["Winv"][:, :], vb_t[:, 0:R])
            pe.transpose(bank[2][:, 2 * R:2 * R + D], w["WO"][:, :], ident[:, :])
            mm(bank[3][:, 0:D], wf[:, 0, :], cos, True, False)
            mm(bank[3][:, 0:D], wf[:, 1, :], sin, False, True)
            mm(bank[3][:, D:2 * D], wf[:, 1, :], cos, True, False)
            mm(bank[3][:, D:2 * D], wf[:, 0, :], nsin, False, True).then_inc(set1, 1)
            with pe.Fori(0, NC // 2) as i:
                for g in range(2):
                    transposes(i, g)
            pe.wait_ge(set1_sb, 1)
            pe.wait_ge(g_const, 3)
            mm(bank[4][:, 0:3 * R], w["WQ"][:, :], vb_t[:, :])
            mm(bank[4][:, 3 * R:6 * R], w["WK"][:, :], wb_t[:, :])
            mm(bank[4][:, 6 * R:8 * R], aT[:, 0, :], cos, True, False)
            mm(bank[4][:, 6 * R:8 * R], aT[:, 1, :], nsin, False, True)
            mm(bank[5][:, 0:D], ub2[:, :], woT[:, :])
            mm(bank[5][0:R, D:2 * D], ut[:, :], woT[:, :])
            mm(bank[5][0:1, 2 * D:3 * D], bb[:, 3:4], woT[:, :])
            for k in range(2):
                for g in range(HG):
                    last = mm(bank[5][:, 3 * D + k * HG + g:3 * D + k * HG + g + 1],
                              brep[0:1, k, 4 * g:4 * g + 4, :].rearrange("p h e -> p (h e)"), ones[0:1, 0:1])
            last.then_inc(set2, 1)
            pe.wait_ge(xT_used, NC + 2)
            for t in range(NT):
                last = mm(bank[0][:, t * E:(t + 1) * E], xnT[:, t * P:(t + 1) * P], Wr[:, :])
            last.then_inc(lg_ps, 1)
            pe.wait_ge(w9_ready, 1)
            for k in range(NC):
                if k >= 4:
                    pe.wait_ge(w9T_ready, k - 3)
                for t in range(4):
                    last = pe.transpose(bank[k % 4][0:E + 1, t * P:(t + 1) * P], w9[:, 4 * k + t, :], ident[:, :])
                last.then_inc(w9_ps, 1)

            pe.wait_ge(set2_sb, 1)
            pe.wait_ge(z_ready, B)
            pe.wait_ge(w9T_ready, NC)
            pe.wait_ge(w1_in, 16 * 4)
            with pe.Fori(0, NC) as c:
                xc, zc = xnT[:, bass.ds(c * C, C)], z[:, bass.ds(c * C, C)]

                def hidden(e):
                    for j in range(2):
                        u = 2 * e + j
                        pe.wait_ge(h_used, c * 2 * E + u + 1)
                        for half in range(2):
                            last = mm(bank[2 * (u % 2) + half][:, :], W1[:, e, half * HF + j * P:half * HF + (j + 1) * P], xc)
                        last.then_inc(h_ps, 1)

                def down(e):
                    pe.wait_ge(h_used, c * 2 * E + 2 * e + 4)
                    pe.wait_ge(y_used, c * E + e + 1)
                    for t in range(4):
                        for j in range(2):
                            last = mm(bank[4 + e % 2][:, t * P:(t + 1) * P], actT[:, e % 2, j, t * P:(t + 1) * P],
                                      W2[:, e, j, :], j == 0, j == 1)
                    last.then_inc(y_ps, 1)

                pe.wait_ge(r_act, c * 2 + 2)
                mm(bank[6][:, :], LQ[:, 0:2 * R], xc).then_inc(r_ps, 1)
                pe.wait_ge(r_dve, c * 4 + 4)
                mm(bank[7][:, :], LK[:, 0:2 * R], zc).then_inc(r_ps, 1)
                pe.wait_ge(r_act, c * 2 + 3)
                pe.sem_inc(apart, 1)
                mm(bank[6][0:R, :], LQ[:, 2 * R:3 * R], xc).then_inc(r_ps, 1)
                pe.wait_ge(r_dve, c * 4 + 5)
                mm(bank[7][:, :], LK[:, 2 * R:4 * R], zc).then_inc(r_ps, 1)
                hidden(0)
                pe.wait_ge(r_dve, c * 4 + 7)
                pe.wait_ge(w9c_ready, c + 1)
                for t in range(4):
                    s = slice(t * P, (t + 1) * P)
                    mm(bank[7][:, s], sB[:, s], UB[:, :], True, False)
                    mm(bank[7][:, s], tri[:, s], UT[:, :], False, False)
                    last = mm(bank[7][:, s], w9c[:, s], b2a[:, :], False, True)
                last.then_inc(r_ps, 1)
                for e in range(1, E):
                    hidden(e)
                    down(e - 1)
                down(E - 1)

            pe.wait_ge(cp_in, 16 * 6)
            pe.wait_ge(identr_ready, 3)
            pe.wait_ge(h_used, NC * 2 * E + 2)
            pe.wait_ge(r_dve, NC * 4 + 4)
            pe.wait_ge(y_used, NC * E + 2)
            with pe.Fori(0, B) as b:
                n = dict.fromkeys(n_of, 0)
                for step in steps:
                    kind, g, i = step
                    if kind in MISC:
                        pe.wait_ge(m_used[misc_at[step] % 2], b * (n_misc // 2) + misc_at[step] // 2 + 1)
                        o = misc_bank(step)
                    if kind == "xT":
                        transposes(b + NC // 2, i)
                    elif kind == "V":
                        if i == 0:
                            pe.wait_ge(xT_used, (b + NC // 2) * 2 + 4)
                        for k, j in enumerate(value_slots(i)):
                            rows = xn2T[:, ST - 1 + C * j:C * (j + 1):ST] if j < 2 else xn2T[:, (j - 2) * P:(j - 1) * P]
                            last = mm(o[:, k * P:(k + 1) * P], rows, cw[:, 2 * D:3 * D])
                        last.then_inc(m_ps, 1)
                    elif kind == "K":
                        mm(o[:, :], wrep[:, i // 2, 4 * g:4 * g + 4, :].rearrange("p h e -> p (h e)"),
                           xn2T[:, (i % 2) * C:(i % 2 + 1) * C]).then_inc(m_ps, 1)
                    elif kind == "A":
                        u = n["A"]
                        t, r = divmod(i, 4)
                        if i == 0:
                            for k in {misc_at["K", g, k] % 2: k for k in range(4)}.values():
                                misc_read(pe, b, ("K", g, k))
                        pe.wait_ge(a_used, b * n_of["A"] + u + 1)
                        rows = slice(32 * r, 32 * r + KQ)
                        q = qs[rows, g % 2, t * P:(t + 1) * P]
                        mm(bank[u % 2][:, 0:NS], q, ks[rows, g % 2, ST - 1:T:ST])
                        mm(bank[u % 2][:, NS:KW], q, ks[rows, g % 2, t * P:(t + 1) * P]).then_inc(a_ps, 1)
                    elif kind == "M":
                        pe.wait_ge(n_ready, b * HG + g + 1)
                        pe.sem_inc(apart, 1)
                        pe.transpose(o[0:8 * TB, 0:P], nm[:, :, :, :].rearrange("p r s t -> p (r s t)"),
                                     ident[:, :]).then_inc(m_ps, 1)
                    elif kind == "S":
                        u = n["S"]
                        qc, r, part = i // 12, i // 3 % 4, PARTS[i % 3]
                        if i == 0:
                            pe.wait_ge(m_rows, (b * HG + g) * 128 + 256)
                        pe.wait_ge(p_ready, b * n_of["S"] + u + 1)
                        o = bank[3 + u % 3]
                        rows = slice(32 * r, 32 * r + KM)
                        q = qs[rows, g % 2, qc * C:(qc + 1) * C]
                        if part < 2:
                            keys = ks[rows, g % 2, ST - 1 + C * part:C * (part + 1):ST]
                            last = mm(o[:, :], keys, q, True, part != qc)
                            if part == qc:
                                last = mm(o[:, :], identr[:, :], mstr_r[:, :], False, True)
                        else:
                            for j in range(4):
                                s = slice(j * P, (j + 1) * P)
                                mm(o[:, s], ks[rows, g % 2, qc * C + j * P:qc * C + (j + 1) * P], q[:, s],
                                   j == 0, False, skip_group_check=True)
                            last = mm(o[:, :].rearrange("p (t k) -> p t k", t=4), identr[:, :],
                                      mloc_r[:, :].unsqueeze(1).broadcast_to([P, 4, P]), False, True,
                                      skip_group_check=True)
                        last.then_inc(s_ps, 1)
                    elif kind == "P":
                        u = n["P"]
                        qc, r, part = i // 12, i // 3 % 4, PARTS[i % 3]
                        pe.wait_ge(p_ready, b * n_of["S"] + u + 4)
                        if i % 12 == 0:
                            pe.wait_ge(on_ready, b * n_of["O"] + 2 * g + qc + 1)
                        o = bank[6][32 * r:32 * r + 32, :]
                        if part < 2:
                            last = mm(o, vaug[:, part, 4 * g + r, :], pT[:, u % 4, :], False, part == 1,
                                      skip_group_check=True)
                        else:
                            for j in range(4):
                                s = slice(j * P, (j + 1) * P)
                                last = mm(o[:, s], vaug[:, 2 + 4 * qc + j, 4 * g + r, :], pT[:, u % 4, s],
                                          j == 0, False, skip_group_check=True)
                        last.then_inc(p_used, 1)
                    elif kind == "O":
                        pe.wait_ge(p_used, b * n_of["S"] + n["P"] + 4)
                        pe.sem_inc(o_ps, 1)
                    elif kind == "D":
                        pe.wait_ge(on_ready, b * n_of["O"] + 2 * g + i + 2)
                        mm(o[:, :], bsel[:, :], onum[:, i, :]).then_inc(m_ps, 1)
                    elif kind == "F":
                        pe.wait_ge(oT_ready, b * n_of["D"] + n_of["D"] - 1 + i + 2)
                        for k in range(4):
                            s = slice(i * C + k * P, i * C + (k + 1) * P)
                            for h in range(HG):
                                mm(o[:, k * P:(k + 1) * P], oT[:, h, s], cp[:, h, :], h == 0, False)
                            last = mm(o[:, k * P:(k + 1) * P], xn2T[:, s], G[:, :], False, True)
                        last.then_inc(m_ps, 1)
                    n[kind] += 1


INS = """L0_attn_x L0_attn_WQ L0_attn_WK L0_attn_WO L0_attn_Winv L0_attn_U_b L0_attn_V_b L0_attn_W_b L0_attn_bias_b
         L0_attn_U_t L0_attn_V_t L0_attn_W_t L0_attn_X_t L0_attn_bias_t L0_attn_alpha_bi L0_attn_alpha_tri
         L0_ffn_W1 L0_ffn_b1 L0_ffn_W2 L0_ffn_b2 L0_ffn_Wr L0_ffn_br
         L1_attn_c_attn_w L1_attn_c_attn_b L1_attn_c_proj_w L1_attn_c_proj_b L1_ffn_w_freq_real L1_ffn_w_freq_imag L1_ffn_bias""".split()


def constants():
    k = np.arange(D)
    angle = 2.0 * np.pi * ((k[:, None] * k[None, :]) % D) / D
    low = np.zeros((P, 2))
    low[:, 0] = k % 32 // HD == 2
    low[:, 1] = k % 32 // HD == 1
    sel = (k[:, None] == k[None, :] // 32 * 32 + HD)
    made = {"dft": np.stack([np.cos(angle), np.sin(angle), -np.sin(angle)], 1), "low_rows": low,
            "rcount": 1.0 / np.arange(1, T + 1), "desc": np.arange(E, 0, -1), "ident": np.eye(P), "bsel": sel}
    return {n: np.ascontiguousarray(v, np.float32) for n, v in made.items()}


def kernel(**inputs):
    import concourse.bacc as bacc
    from concourse.bass_utils import run_bass_kernel_spmd

    nc = bacc.Bacc("TRN2", target_bir_lowering=False, num_devices=1)
    arrays, args = {}, {}
    for name in INS:
        v = np.asarray(inputs[name])
        if name == "L0_ffn_b1":
            v = v.reshape(E, 2 * HF // P, P).transpose(2, 1, 0)
        arrays[name + "_dram"] = np.ascontiguousarray(v.reshape(v.shape or (1,)))
    for name, v in constants().items():
        arrays[name + "_dram"] = v
    for name, v in arrays.items():
        args[name[:-5]] = nc.dram_tensor(name, v.shape, mybir.dt.from_np(v.dtype), kind="ExternalInput").ap()
    out = nc.dram_tensor("out_dram", (B, T, D), F32, kind="ExternalOutput").ap()
    build(nc, args, out)
    got = run_bass_kernel_spmd(nc, [arrays], core_ids=[0])
    return got.results[0]["out_dram"]
```

```python
from contextlib import ExitStack

import numpy as np

import concourse.bass as bass
from concourse import mybir

F32 = mybir.dt.float32
F32R = mybir.dt.float32r
ALU = mybir.AluOpType
ACT = mybir.ActivationFunctionType
AX = mybir.AxisListType

B, T, D, R = 4, 1024, 128, 64
P = 128
NT = B * T // P
TB = T // P
C = 512
NC = B * T // C
E, HF = 8, 256
NH, HD = 16, 8
HG = 4
ST = 4
NS = T // ST
KW = NS + P
MASK = -10000.0
FAR = -1.0e38
EPS = 1e-5
KQ = 3 * HD
KM = KQ + 2

WEIGHTS = ["WQ", "WK", "WO", "Winv"]
THIN = ["U_b", "V_b", "W_b", "U_t", "V_t", "W_t", "X_t"]


class Chain:

    def __init__(self, eng, sem):
        self.eng, self.sem, self.n, self.turn, self.count = eng, sem, 0, None, 0

    def loop(self, turn, count):
        self.turn, self.count, self.at = turn, count, self.n

    def done(self, turns):
        assert self.n - self.at == self.count, (self.n - self.at, self.count)
        self.n, self.turn = self.at + turns * self.count, None

    def __call__(self, ins):
        self.n += 1
        ins.then_inc(self.sem, 1)
        self.eng.wait_ge(self.sem, self.n if self.turn is None else self.turn * self.count + self.n)


MISC = "XVKMYTUF"
MB = (2, 7)
N_LOADS = 32
PARTS = (2, 0, 1)


def layer1_steps():
    def turn(last):
        steps, n_a = [], 24
        for g in range(HG):
            side = not (last and g == HG - 1)
            nb, ng = (g + 1) // HG, (g + 1) % HG
            for i in range(24):
                more = []
                while i < 6 and n_a < 32 and (n_a - 24) * 3 < (i + 1) * 4:
                    more.append(("A", 0, g, n_a))
                    n_a += 1
                if i == 6:
                    more += [("N", 0, g, 1), ("M", 0, g, 1)]
                    n_a = 0
                while i >= 6 and side and n_a < 24 and n_a * 3 < (i - 5) * 4:
                    more.append(("A", nb, ng, n_a))
                    n_a += 1
                steps.append(("S", 0, g, i))
                steps += more
                if i >= 7 and i % 4 == 3:
                    steps += [("P", 0, g, j) for j in range(i - 7, i - 3)]
                if i == 15:
                    steps.append(("O", 0, g, 0))
                if i == 19:
                    steps.append(("T", 0, g, 0))
                if g and i == 4:
                    steps.append(("T", 0, g - 1, 1))
                if side and i < 4:
                    steps.append(("K", nb, ng, i))
                if side and i == 18:
                    steps += [("N", nb, ng, 0), ("M", nb, ng, 0)]
                if g == HG - 2 and i in (8, 11):
                    steps.append(("Y", 0, 0, int(i > 8)))
                if g == HG - 2 and not last and i in (14, 17):
                    steps.append(("X", 1, 0, int(i > 14)))
                if g == HG - 1 and i in (21, 23):
                    steps.append(("UF"[i > 21], 0, 0, 0))
            steps += [("P", 0, g, j) for j in range(20, 24)] + [("O", 0, g, 1)]
        tail = [("T", 0, HG - 1, 1), ("U", 0, 0, 1), ("F", 0, 0, 1)]
        if not last:
            v = [("V", 1, 0, js) for js in ((0, 3), (3, 6), (6, 8), (8, 10))]
            return steps + v[:2] + tail[:1] + v[2:3] + tail[1:2] + v[3:] + tail[2:]
        return steps + tail

    first = [("X", 0, 0, 0), ("X", 0, 0, 1)] + [("V", 0, 0, js) for js in ((0, 4), (4, 8), (8, 10))]
    first += [("K", 0, 0, i) for i in range(4)] + [("A", 0, 0, i) for i in range(24)]
    return first + [("N", 0, 0, 0), ("M", 0, 0, 0)], turn(False), turn(True)


class Walk:

    def __init__(self):
        self.before, self.per = dict.fromkeys(KINDS, 0), dict.fromkeys(KINDS, 0)
        self.turn = 0
        self.batch = 0

    def no(self, kind, of=1):
        assert self.per[kind] % of == 0 and self.before[kind] % of == 0
        return self.turn * (self.per[kind] // of) + self.before[kind] // of

    def misc(self):
        return sum(self.before[k] for k in MISC) % 2

    def misc_no(self):
        return self.turn * sum(self.per[k] for k in MISC) + sum(self.before[k] for k in MISC)

    def misc_fills(self):
        return self.turn * (sum(self.per[k] for k in MISC) // 2) + sum(self.before[k] for k in MISC) // 2

    def take(self, steps, do):
        for step in steps:
            do(self, *step)
            self.before[step[0]] += 1

    def run(self, eng, do):
        first, turn, last = layer1_steps()
        self.take(first, do)
        start, per = dict(self.before), {k: sum(s[0] == k for s in turn) for k in KINDS}
        assert sum(start[k] for k in MISC) % 2 == 0 and sum(per[k] for k in MISC) % 2 == 0
        with eng.Fori(0, B - 1) as b:
            self.turn, self.batch, self.per = b, b, per
            self.take(turn, do)
        self.turn, self.batch = 0, B - 1
        self.before = {k: start[k] + (B - 1) * per[k] for k in KINDS}
        self.take(last, do)


KINDS = "XVKANMSPOTUYF"


def build(nc, a, out):
    x_d = a["L0_attn_x"].rearrange("b (t p) d -> p (b t) d", p=P)
    out_d = out.rearrange("b (t p) d -> b p t d", p=P)
    with ExitStack() as ctx:
        def sb(name, shape, dt=F32, scope=ctx):
            return scope.enter_context(nc.sbuf_tensor(name, shape, dt))

        def sem(name):
            return ctx.enter_context(nc.semaphore(name))

        bank = [ctx.enter_context(nc.psum_tensor(f"bank{i}", [P, C], F32)) for i in range(8)]

        x = sb("x_tok", [P, NT, D])
        tokens_a = sb("tokens_a", [P, 2 * B * T])
        weights_a = sb("weights_a", [P, 3 * E * 2 * D])
        routing_a = sb("routing_a", [P, B * T])
        xnT = tokens_a[:, 0:B * T]
        z = tokens_a[:, B * T:2 * B * T]
        xst = sb("xst", [P, 2, 4, D])
        stats = sb("stats", [P, NT, 6])
        ln = sb("ln", [P, 10, NT])
        MEAN, RSTD = 0, 1
        ident = sb("ident", [P, P])
        identr = sb("identr", [P, P], F32R)
        ones = sb("ones", [P, T])
        al = sb("al", [P, 4])
        bb = sb("bb", [P, 4])
        G = sb("G", [P, D])
        W1 = weights_a[:, 0:E * 2 * HF].rearrange("p (e h) -> p e h", e=E)
        b1 = sb("b1", [P, 2 * HF // P, E])
        W2 = weights_a[:, E * 2 * HF:E * 3 * HF].rearrange("p (e k d) -> p e k d", e=E, k=2)
        b2a = sb("b2a", [E + 1, D])
        Wr = sb("Wr", [P, E])
        brb = sb("brb", [P, E])
        gs = sb("gs", [P, 4, NT])
        desc = sb("desc", [P, E])
        w9 = sb("w9", [P, NT, E + 1])
        w9T = routing_a[0:E + 1, :]
        cw = sb("cw", [P, 3 * D])
        cb = sb("cb", [1, 3 * D])
        wrep = sb("wrep", [P, 2, NH, 32])
        brep = sb("brep", [1, 2, NH, 32])
        bqk = sb("bqk", [P, 2, HG])
        bqk_low = sb("bqk_low", [P, 2, HG])
        lowm = sb("lowm", [P, 2])
        bvb = sb("bvb", [P, D])
        cproj = sb("cproj", [P, D])
        bias2 = sb("bias2", [2, D])
        mask1 = routing_a[:, 0:TB * KW].rearrange("p (t k) -> p t k", t=TB)
        mstr = sb("mstr", [P, C])
        mloc = sb("mloc", [P, P])
        mstr_r = sb("mstr_r", [P, C], F32R)
        mloc_r = sb("mloc_r", [P, P], F32R)
        maskc = sb("maskc", [P, 2])
        NV = (2 + TB) * NH * (HD + 1)
        vaug = tokens_a[:, 0:NV].rearrange("p (j h e) -> p j h e", h=NH, e=HD + 1)
        qz = sb("qz", [P, 2, 4, T], F32R)
        junk = routing_a[:, TB * KW:(TB + 2) * KW].rearrange("p (t k) -> p t k", t=2)
        rd = sb("rd", [P, 2, 16])
        mx = sb("mx", [P, 2, 4, TB])
        nm = sb("nm", [P, 2, 4, 2, TB // 2])
        nmr = sb("nmr", [P, 4, TB // 2], F32R)
        mT = sb("mT", [4 * TB, 2, P], F32R)
        pT = tokens_a[:, NV:NV + 8 * C].rearrange("p (u q) -> p u q", u=8)
        onum = tokens_a[:, NV + 8 * C:NV + 10 * C].rearrange("p (u q) -> p u q", u=2)
        on = weights_a[:, 0:TB * D].rearrange("p (t d) -> p t d", t=TB)
        oT = weights_a[:, TB * D:TB * D + T].rearrange("p (u q) -> p u q", u=2)
        yo = weights_a[:, 2 * T:2 * T + 2 * C].rearrange("p (u t d) -> p u t d", u=2, t=4)
        layer0 = ExitStack()
        rcount = sb("rcount", [P, T], scope=layer0)
        w = {n: sb("w_" + n, [P, D], scope=layer0) for n in WEIGHTS}
        vb_t = sb("rq", [P, 3 * R], scope=layer0)
        wb_t = sb("rk", [P, 3 * R], scope=layer0)
        ub2 = sb("ub2", [P, 2 * R], scope=layer0)
        ut = sb("ut", [P, R], scope=layer0)
        LQ = sb("LQ", [P, 3 * R], scope=layer0)
        LK = sb("LK", [P, 4 * R], scope=layer0)
        UB = sb("UB", [P, D], scope=layer0)
        UT = sb("UT", [R, D], scope=layer0)
        woT = sb("woT", [P, D], scope=layer0)
        dft = sb("dft", [P, 3, D], scope=layer0)
        wf = sb("wf", [P, 2, D], scope=layer0)
        aT = sb("aT", [P, 2, D], scope=layer0)
        lg = sb("lg", [P, NT, E], scope=layer0)
        gt = sb("gt", [P, 4, NT, E], scope=layer0)
        w9c = sb("w9c", [E + 1, C], scope=layer0)
        sa = sb("sa", [P, C], scope=layer0)
        sB = sb("sB", [P, C], scope=layer0)
        sc = sb("sc", [R, C], scope=layer0)
        tc = sb("tc", [R, C], scope=layer0)
        tri = sb("tri", [R, C], scope=layer0)
        sil = sb("sil", [P, 2, C], scope=layer0)
        actT = sb("actT", [P, 2, 2, C], scope=layer0)
        yw = sb("yw", [P, 2, 4, D], scope=layer0)
        layer0.close()
        xn2T = sb("xn2T", [P, T])
        kt = sb("kt", [P, 2, C])
        hp = sb("hp", [P, 2, C], F32R)
        qs = sb("qs", [P, T], F32R)
        ks = sb("ks", [P, 2, T], F32R)

        x_in = [sem(f"x_in{b}") for b in range(B)]
        w_in, w1_in = sem("w_in"), sem("w1_in")
        g_const = sem("g_const")
        g_chain, d_chain = sem("g_chain"), sem("d_chain")
        var_ready, sq_ready = sem("var_ready"), sem("sq_ready")
        xn_ready, xT_done, xT_used = sem("xn_ready"), sem("xT_done"), sem("xT_used")
        z_sum, z_ready = sem("z_sum"), sem("z_ready")
        set1, set1_sb, set2, set2_sb = sem("set1"), sem("set1_sb"), sem("set2"), sem("set2_sb")
        identr_ready = sem("identr_ready")
        lg_ps, dif_ready, exp_ready, w9_ready = sem("lg_ps"), sem("dif_ready"), sem("exp_ready"), sem("w9_ready")
        w9_ps, w9T_ready = sem("w9_ps"), sem("w9T_ready")
        r_ps, r_act, r_dve = sem("r_ps"), sem("r_act"), sem("r_dve")
        h_ps, sil_ready, h_used = sem("h_ps"), sem("sil_ready"), sem("h_used")
        y_ps, y_used, yw_used = sem("y_ps"), sem("y_used"), sem("yw_used")
        w9c_ready = sem("w9c_ready")
        m_ps, m_used = sem("m_ps"), [sem("m_used0"), sem("m_used1")]
        kt_ready, hp_ready, qk_ready = sem("kt_ready"), sem("hp_ready"), sem("qk_ready")
        a_ps, a_used = sem("a_ps"), sem("a_used")
        q_rows, qz_clear = sem("q_rows"), sem("qz_clear")
        n_part, n_ready, m_rows = sem("n_part"), sem("n_ready"), sem("m_rows")
        s_ps, p_ready, p_used = sem("s_ps"), sem("p_ready"), sem("p_used")
        on_ready, rd_ready, o_clear = sem("on_ready"), sem("rd_ready"), sem("o_clear")
        apart = sem("apart")
        out_done = [sem(f"out_done{i}") for i in range(2)]

        block = ctx.enter_context(nc.Block())


        def misc_full(eng, w):
            eng.wait_ge(m_ps, w.misc_no() + 1)

        def misc_read(eng, w):
            eng.wait_ge(m_used[w.misc()], w.misc_fills() + 2)

        @block.sync
        def _(sp):
            for b in range(B):
                sp.dma_start(x[:, b * TB:(b + 1) * TB, :], x_d[:, b * TB:(b + 1) * TB, :]).then_inc(x_in[b], 16)
            sp.dma_start(W1[:, :, :], a["L0_ffn_W1"].rearrange("e d h -> d e h")).then_inc(w1_in, 16)
            for k in range(2):
                sp.dma_start(W2[:, :, k, :], a["L0_ffn_W2"][:, k * P:(k + 1) * P, :].rearrange("e p d -> p e d")).then_inc(w1_in, 16)
            sp.dma_start(b1[:, :, :], a["L0_ffn_b1"]).then_inc(w1_in, 16)

            def layer1(w, kind, ahead, g, i):
                if kind == "K" and i == 1:
                    sp.wait_ge(qk_ready, w.no("K") + 3)
                    for r in range(4):
                        rows = slice(32 * r, 32 * r + 32)
                        sp.dma_start(qz[rows, g % 2, r, :].bitcast(F32), qs[rows, :].bitcast(F32)).then_inc(q_rows, 16)
                elif kind == "M":
                    misc_read(sp, w)
                    for r in range(4):
                        for s in range(2):
                            row = (r * 2 + s) * TB // 2
                            sp.dma_start(qz[32 * r + KQ + s:32 * r + KQ + s + 1, g % 2, r, i * C:(i + 1) * C].bitcast(F32),
                                         mT[row:row + TB // 2, i, :].bitcast(F32)).then_inc(m_rows, 16)
                elif kind == "F":
                    misc_read(sp, w)
                    sp.dma_start(out_d[bass.ds(w.batch, 1), :, 4 * i:4 * i + 4, :].rearrange("a p t d -> (a p) t d"),
                                 yo[:, i, :, :]).then_inc(out_done[i], 16)

            sp.wait_ge(qz_clear, 1)
            Walk().run(sp, layer1)
            for k in range(2):
                sp.wait_ge(out_done[k], 16 * (B + 1))

        @block.scalar
        def _(act):
            act.sem_inc(r_act, 2)
            act.sem_inc(xT_used, 2)
            act.sem_inc(out_done[0], 16)
            act.sem_inc(out_done[1], 16)
            act.sem_inc(p_ready, 3)
            act.sem_inc(on_ready, 1)
            loads = [(w[k][:, :], a["L0_attn_" + k]) for k in WEIGHTS]
            loads += [(vb_t[:, 0:R], a["L0_attn_V_b"]), (vb_t[:, 2 * R:3 * R], a["L0_attn_V_t"]),
                      (wb_t[:, 0:R], a["L0_attn_W_b"]), (wb_t[:, 2 * R:3 * R], a["L0_attn_W_t"]),
                      (ub2[:, 0:R], a["L0_attn_U_b"]), (ub2[:, R:2 * R], a["L0_attn_U_b"]),
                      (ut[:, :], a["L0_attn_U_t"]), (LK[:, 3 * R:4 * R], a["L0_attn_X_t"]),
                      (al[:, 0:1], a["L0_attn_alpha_bi"].partition_broadcast(P)),
                      (al[:, 1:2], a["L0_attn_alpha_tri"].partition_broadcast(P)),
                      (bb[:, 0:1], a["L0_attn_bias_b"].rearrange("(p a) -> p a", a=1)),
                      (bb[:, 1:2], a["L0_attn_bias_t"].rearrange("(p a) -> p a", a=1)),
                      (dft[:, :, :], a["dft"]), (wf[:, 0, :], a["L1_ffn_w_freq_real"]),
                      (wf[:, 1, :], a["L1_ffn_w_freq_imag"]), (b2a[1:E + 1, :], a["L0_ffn_b2"]),
                      (Wr[:, :], a["L0_ffn_Wr"]), (brb[:, :], a["L0_ffn_br"].partition_broadcast(P)),
                      (cw[:, :], a["L1_attn_c_attn_w"]),
                      (cb[:, :], a["L1_attn_c_attn_b"].rearrange("(a n) -> a n", a=1)),
                      (bvb[:, :], a["L1_attn_c_attn_b"][2 * D:3 * D].partition_broadcast(P)),
                      (lowm[:, :], a["low_rows"]), (rcount[:, :], a["rcount"].partition_broadcast(P)),
                      (desc[:, :], a["desc"].partition_broadcast(P)), (ident[:, :], a["ident"]),
                      (cproj[:, :], a["L1_attn_c_proj_w"]),
                      (bias2[0:1, :], a["L1_attn_c_proj_b"].rearrange("(a n) -> a n", a=1)),
                      (bias2[1:2, :], a["L1_ffn_bias"].rearrange("(a n) -> a n", a=1))]
            assert len(loads) == N_LOADS
            for dst, src in loads:
                act.dma_start(dst, src).then_inc(w_in, 16)
            def root(n):
                act.wait_ge(var_ready, n)
                nc.scalar.activation(ln[:, 2, :], ln[:, 1, :], ACT.Sqrt).then_inc(sq_ready, 1)

            def xT_out(dst, turn, g):
                act.wait_ge(xT_done, turn * 2 + g + 3)
                nc.scalar.activation(dst, bank[g][:, :], ACT.Copy).then_inc(xT_used, 1)

            root(1)
            with act.Fori(0, NC // 2) as i:
                for g in range(2):
                    xT_out(xnT[:, bass.ds(i * 2 * C + g * C, C)], i, g)
            act.wait_ge(w_in, 16 * N_LOADS)
            nc.scalar.activation(identr[:, :], ident[:, :], ACT.Copy).then_inc(identr_ready, 1)
            act.wait_ge(g_const, 1)
            nc.scalar.activation(mstr_r[:, :], mstr[:, :], ACT.Copy).then_inc(identr_ready, 1)
            nc.scalar.activation(mloc_r[:, :], mloc[:, :], ACT.Copy).then_inc(identr_ready, 1)
            act.wait_ge(dif_ready, 1)
            nc.scalar.activation(gs[:, 3, :], gs[:, 2, :], ACT.Exp).then_inc(exp_ready, 1)
            for k in range(NC):
                act.wait_ge(w9_ps, k + 1)
                nc.scalar.activation(w9T[:, k * C:(k + 1) * C], bank[k % 4][0:E + 1, :], ACT.Copy).then_inc(w9T_ready, 1)

            act.wait_ge(w1_in, 16 * 4)
            with act.Fori(0, NC) as c:
                act.wait_ge(r_ps, c * 5 + 1)
                act.wait_ge(r_dve, c * 4 + 1)
                nc.scalar.activation(sa[:, :], bank[6][:, :], ACT.Copy).then_inc(r_act, 1)
                act.wait_ge(r_ps, c * 5 + 3)
                act.wait_ge(r_dve, c * 4 + 2)
                nc.scalar.activation(sc[:, :], bank[6][0:R, :], ACT.Copy).then_inc(r_act, 1)
                for e in range(E):
                    for j in range(2):
                        u = 2 * e + j
                        act.wait_ge(h_ps, c * 2 * E + u + 1)
                        act.wait_ge(h_used, c * 2 * E + u + 1)
                        nc.scalar.activation(sil[:, u % 2, :], bank[2 * (u % 2)][:, :], ACT.Silu,
                                             bias=b1[:, j, e:e + 1]).then_inc(sil_ready, 1)

            root(2)

            def layer1(w, kind, ahead, g, i):
                if kind in "XU":
                    misc_full(act, w)
                    dst = xn2T[:, i * C:(i + 1) * C] if kind == "X" else oT[:, i, :]
                    nc.scalar.activation(dst, bank[MB[w.misc()]][:, :], ACT.Copy).then_inc(m_used[w.misc()], 1)
                elif kind == "K":
                    misc_full(act, w)
                    act.wait_ge(qk_ready, w.no("K") + 1)
                    n, k = w.before["K"] % 2, i // 2
                    nc.scalar.activation(hp[:, n, :], bank[MB[w.misc()]][:, :], ACT.Identity,
                                         bias=bqk_low[:, k, g:g + 1], scale=lowm[:, k:k + 1]).then_inc(hp_ready, 1)
                    nc.scalar.activation(kt[:, n, :], bank[MB[w.misc()]][:, :], ACT.Identity,
                                         bias=bqk[:, k, g:g + 1]).then_inc(m_used[w.misc()], 1)
                elif kind == "M":
                    misc_full(act, w)
                    act.wait_ge(m_rows, w.no("M") * 128 + 128)
                    nc.scalar.activation(mT[:, i, :], bank[MB[w.misc()]][0:4 * TB, 0:P],
                                         ACT.Copy).then_inc(m_used[w.misc()], 1)
                elif kind == "S":
                    u = w.before["S"]
                    act.wait_ge(s_ps, w.no("S") + 1)
                    act.wait_ge(p_used, w.no("S") + 1)
                    later = (PARTS[i % 12 // 4], i // 12) == (1, 0)
                    nc.scalar.activation(pT[:, u % 8, :], bank[3 + u % 3][:, :], ACT.Exp,
                                         bias=maskc[:, 0:1] if later else 0.0).then_inc(p_ready, 1)
                elif kind == "O":
                    act.wait_ge(p_used, w.no("P") + 8)
                    nc.scalar.activation(onum[:, i, :], bank[6][:, :], ACT.Copy).then_inc(on_ready, 1)

            Walk().run(act, layer1)

        @block.gpsimd
        def _(pool):
            pool.sem_inc(yw_used, 2)
            pool.sem_inc(qk_ready, 2)
            pool.sem_inc(m_rows, 128)
            pool.sem_inc(q_rows, 64)
            link = Chain(pool, g_chain)
            nc.gpsimd.memset(ones[:, :], 1.0)
            nc.gpsimd.memset(qz[:, :, :, :].bitcast(F32), 0.0).then_inc(qz_clear, 1)
            nc.gpsimd.memset(maskc[:, :], MASK)
            nc.gpsimd.memset(w9[:, :, 0:1], 1.0)
            nc.gpsimd.memset(mstr[:, :], 0.0)
            link(nc.gpsimd.memset(mloc[:, :], 0.0))
            nc.gpsimd.memset(wrep[:, :, :, :], 0.0)
            nc.gpsimd.memset(brep[:, :, :, :], 0.0)
            nc.gpsimd.affine_select(out=mstr[:, :], in_=mstr[:, :], compare_op=ALU.is_ge, fill=MASK,
                                    base=-(ST - 1), pattern=[[1, C]], channel_multiplier=-ST)
            link(nc.gpsimd.affine_select(out=mloc[:, :], in_=mloc[:, :], compare_op=ALU.is_ge, fill=MASK,
                                         base=0, pattern=[[1, P]], channel_multiplier=-1))
            for lo, other in ((0, 64), (64, 0)):
                last = nc.gpsimd.memset(mloc[lo:lo + 64, other:other + 64], FAR)
            link(last)
            link(nc.gpsimd.memset(brep[:, 1, :, KQ:KM], 1.0))
            pool.sem_inc(g_const, 1)
            pool.wait_ge(w_in, 16 * N_LOADS)
            scale = float(np.float32(1) / np.sqrt(np.float32(HD)))
            for src, dst in ((cw, wrep), (cb, brep)):
                for s in range(3):
                    for k in range(2):
                        last = nc.gpsimd.tensor_scalar(dst[:, k, :, s * HD:(s + 1) * HD],
                                                       src[:, k * D:(k + 1) * D].rearrange("p (h e) -> p h e", h=NH),
                                                       scale if k == 0 else 1.0, None, ALU.mult)
            last.then_inc(g_const, 1)
            for b in range(B):
                pool.wait_ge(z_sum, b + 1)
                nc.gpsimd.tensor_tensor(z[:, b * T:(b + 1) * T], z[:, b * T:(b + 1) * T], rcount[:, :],
                                        ALU.mult).then_inc(z_ready, 1)
            pool.wait_ge(w9T_ready, NC)
            with pool.Fori(0, NC) as c:
                pool.wait_ge(r_dve, c * 4 + 4)
                nc.gpsimd.tensor_copy(w9c[:, :], w9T[:, bass.ds(c * C, C)]).then_inc(w9c_ready, 1)
                pool.wait_ge(r_dve, c * 4 + 8)
                for e in range(E):
                    pool.wait_ge(y_used, c * E + e + 3)
                    pool.wait_ge(yw_used, c * E + e + 2)
                    pool.sem_inc(apart, 1)
                    xs = x[:, bass.ds(c * 4, 4), :]
                    nc.gpsimd.tensor_tensor(xs, xs, yw[:, e % 2, :, :], ALU.add).then_inc(yw_used, 1)
            nc.gpsimd.memset(vaug[:, :, :, HD:HD + 1], 1.0)
            link(nc.gpsimd.memset(mask1, 0.0))
            nc.gpsimd.affine_select(out=mask1[:, :, 0:NS], in_=mask1[:, :, 0:NS], compare_op=ALU.is_ge, fill=MASK,
                                    base=-(ST - 1), pattern=[[P, TB], [-ST, NS]], channel_multiplier=1)
            last = nc.gpsimd.affine_select(out=mask1[:, :, NS:KW], in_=mask1[:, :, NS:KW], compare_op=ALU.is_ge, fill=MASK,
                                           base=0, pattern=[[0, TB], [-1, P]], channel_multiplier=1)
            link(last)
            for lo, other in ((0, 64), (64, 0)):
                last = nc.gpsimd.memset(mask1[lo:lo + 64, :, NS + other:NS + other + 64], FAR)
            last.then_inc(g_const, 1)

            def layer1(w, kind, ahead, g, i):
                if kind == "K":
                    k, n = i // 2, w.before["K"] % 2
                    misc_read(pool, w)
                    dst = ks[:, g % 2, :] if k else qs
                    pool.sem_inc(apart, 1)
                    if i == 0:
                        pool.wait_ge(q_rows, w.no("K", 4) * 64 + 64)
                        pool.sem_inc(apart, 1)
                    nc.gpsimd.tensor_tensor(dst[:, (i % 2) * C:(i % 2 + 1) * C], kt[:, n, :],
                                            hp[:, n, :].bitcast(F32), ALU.subtract).then_inc(qk_ready, 1)

            Walk().run(pool, layer1)

        @block.vector
        def _(dve):
            dve.sem_inc(r_dve, 4)
            dve.sem_inc(h_used, 2)
            dve.sem_inc(y_used, 2)
            dve.sem_inc(a_used, 2)
            dve.sem_inc(m_used[0], 1)
            dve.sem_inc(m_used[1], 1)
            link = Chain(dve, d_chain)
            V = nc.vector

            def layer_norm(turn):
                even, odd = stats[:, :, 1], stats[:, :, 4]
                mean, var, sd, s0, s1, rstd = (ln[:, k, :] for k in (0, 1, 2, 3, 4, 5))
                V.tensor_tensor(s0, even, odd, ALU.add)
                V.tensor_tensor(s1, even, odd, ALU.subtract)
                link(V.tensor_tensor(var, stats[:, :, 2], stats[:, :, 5], ALU.add))
                V.tensor_scalar(mean, s0, 0.5, None, ALU.mult)
                V.tensor_scalar(var, var, 1.0 / D, EPS, ALU.mult, ALU.add)
                link(V.tensor_tensor(s1, s1, s1, ALU.mult))
                V.scalar_tensor_tensor(out=var, in0=s1, scalar=0.25, in1=var, op0=ALU.mult, op1=ALU.add).then_inc(var_ready, 1)
                dve.wait_ge(sq_ready, turn)
                link(V.reciprocal(rstd, sd))
                link(V.tensor_tensor(s0, rstd, rstd, ALU.mult))
                link(V.tensor_tensor(s0, s0, var, ALU.mult))
                link(V.tensor_scalar(s0, s0, -0.5, 1.5, ALU.mult, ALU.add))
                link(V.tensor_tensor(rstd, rstd, s0, ALU.mult))

            def normalise(tile, g):
                for t in range(4):
                    last = V.tensor_scalar(xst[:, g, t, :], x[:, tile(4 * g + t), :].rearrange("p a d -> p (a d)"),
                                           ln[:, 0, tile(4 * g + t)], ln[:, 5, tile(4 * g + t)],
                                           ALU.subtract, ALU.mult)
                last.then_inc(xn_ready, 1)

            for b in range(B):
                dve.wait_ge(x_in[b], 16)
                with dve.Fori(0, TB) as t:
                    V.bn_stats(stats[:, bass.ds(t + b * TB, 1), :].rearrange("p a s -> p (a s)"),
                               x[:, bass.ds(t + b * TB, 1), :].rearrange("p a d -> p (a d)"))
            link(V.memset(al[:, 2:3], 1.0))
            layer_norm(1)
            with dve.Fori(0, NC // 2) as i:
                for g in range(2):
                    dve.wait_ge(xT_done, i * 2 + g + 1)
                    normalise(lambda t: bass.ds(i * 8 + t, 1), g)

            dve.wait_ge(set1, 1)
            V.tensor_copy(vb_t[:, R:2 * R], bank[2][:, 0:R])
            V.tensor_copy(wb_t[:, R:2 * R], bank[2][:, R:2 * R])
            V.tensor_copy(woT[:, :], bank[2][:, 2 * R:2 * R + D])
            V.tensor_scalar(aT[:, :, :], bank[3][:, 0:2 * D].rearrange("p (k n) -> p k n", k=2), 1.0 / D, None, ALU.mult)
            V.tensor_copy(al[R:2 * R, 2:3], al[R:2 * R, 0:1])
            link(V.scalar_tensor_tensor(out=bb[:, 2:3], in0=bb[:, 0:1], scalar=al[:, 0:1], in1=bb[:, 0:1],
                                        op0=ALU.mult, op1=ALU.add))
            V.scalar_tensor_tensor(out=bb[:, 3:4], in0=bb[:, 1:2], scalar=al[:, 1:2], in1=bb[:, 2:3],
                                   op0=ALU.mult, op1=ALU.add).then_inc(set1_sb, 1)
            dve.wait_ge(g_const, 1)
            dve.wait_ge(xT_used, NC + 2)
            for b in range(B):
                V.tensor_tensor_scan(z[:, b * T:(b + 1) * T], ones[:, :], xnT[:, b * T:(b + 1) * T], 0.0,
                                     ALU.mult, ALU.add).then_inc(z_sum, 1)
            dve.wait_ge(set2, 1)
            V.tensor_copy(LQ[:, :], bank[4][:, 0:3 * R])
            V.tensor_copy(LK[:, 0:3 * R], bank[4][:, 3 * R:6 * R])
            V.tensor_copy(G[:, :], bank[4][:, 6 * R:8 * R])
            V.tensor_scalar(UB[:, :], bank[5][:, 0:D], al[:, 2:3], None, ALU.mult)
            V.tensor_scalar(UT[:, :], bank[5][0:R, D:2 * D], al[0:R, 1:2], None, ALU.mult)
            V.tensor_copy(b2a[0:1, :], bank[5][0:1, 2 * D:3 * D])
            for k in range(2):
                V.tensor_scalar(bqk_low[:, k, :], bank[5][:, 3 * D + k * HG:3 * D + (k + 1) * HG], lowm[:, k:k + 1],
                                None, ALU.mult)
            V.tensor_copy(bqk[:, :, :], bank[5][:, 3 * D:3 * D + 8].rearrange("p (k g) -> p k g", k=2)).then_inc(set2_sb, 1)

            dve.wait_ge(lg_ps, 1)
            wide = [P, NT, E]
            link(V.tensor_tensor(lg[:, :, :], bank[0][:, 0:NT * E].rearrange("p (t e) -> p t e", t=NT),
                                 brb[:, :].unsqueeze(1).broadcast_to(wide), ALU.add))

            def top(logits, hot, best, tmp):
                link(V.tensor_reduce(best, logits, AX.X, ALU.max))
                link(V.tensor_tensor(hot, logits, best.unsqueeze(2).broadcast_to(wide), ALU.is_equal))
                link(V.tensor_tensor(hot, hot, desc[:, :].unsqueeze(1).broadcast_to(wide), ALU.mult))
                link(V.tensor_reduce(tmp, hot, AX.X, ALU.max))
                link(V.tensor_tensor(hot, hot, tmp.unsqueeze(2).broadcast_to(wide), ALU.is_equal))

            top(lg[:, :, :], gt[:, 0, :, :], gs[:, 0, :], gs[:, 3, :])
            link(V.scalar_tensor_tensor(out=gt[:, 1, :, :], in0=gt[:, 0, :, :], scalar=-3.0e38, in1=lg[:, :, :],
                                        op0=ALU.mult, op1=ALU.add))
            top(gt[:, 1, :, :], gt[:, 2, :, :], gs[:, 1, :], gs[:, 3, :])
            V.tensor_tensor(gs[:, 2, :], gs[:, 1, :], gs[:, 0, :], ALU.subtract).then_inc(dif_ready, 1)
            dve.wait_ge(exp_ready, 1)
            link(V.tensor_scalar(gs[:, 0, :], gs[:, 3, :], 1.0, None, ALU.add))
            link(V.reciprocal(gs[:, 1, :], gs[:, 0, :]))
            link(V.tensor_tensor(gs[:, 2, :], gs[:, 3, :], gs[:, 1, :], ALU.mult))
            V.tensor_tensor(gt[:, 0, :, :], gt[:, 0, :, :], gs[:, 1, :].unsqueeze(2).broadcast_to(wide), ALU.mult)
            link(V.tensor_tensor(gt[:, 2, :, :], gt[:, 2, :, :], gs[:, 2, :].unsqueeze(2).broadcast_to(wide), ALU.mult))
            V.tensor_tensor(w9[:, :, 1:E + 1], gt[:, 0, :, :], gt[:, 2, :, :], ALU.add).then_inc(w9_ready, 1)

            with dve.Fori(0, NC) as c:
                xs = x[:, bass.ds(c * 4, 4), :]

                def weigh(e):
                    dve.wait_ge(y_ps, c * E + e + 1)
                    dve.wait_ge(yw_used, c * E + e + 1)
                    V.tensor_tensor(yw[:, e % 2, :, :], bank[4 + e % 2][:, :].rearrange("p (t d) -> p t d", t=4),
                                    w9[:, bass.ds(c * 4, 4), e + 1:e + 2].broadcast_to([P, 4, D]),
                                    ALU.mult).then_inc(y_used, 1)

                dve.wait_ge(r_ps, c * 5 + 2)
                dve.wait_ge(r_act, c * 2 + 3)
                V.tensor_tensor(sB[:, :], sa[:, :], bank[7][:, :], ALU.mult).then_inc(r_dve, 1)
                dve.wait_ge(r_ps, c * 5 + 4)
                dve.wait_ge(r_act, c * 2 + 4)
                V.tensor_tensor(tc[:, :], sc[:, :], bank[7][0:R, :], ALU.mult).then_inc(r_dve, 1)
                dve.wait_ge(r_dve, c * 4 + 6)
                V.tensor_tensor(tri[:, :], tc[:, :], bank[7][R:2 * R, :], ALU.mult).then_inc(r_dve, 1)
                for e in range(E):
                    for j in range(2):
                        u = 2 * e + j
                        dve.wait_ge(sil_ready, c * 2 * E + u + 1)
                        V.scalar_tensor_tensor(out=actT[:, e % 2, j, :], in0=bank[2 * (u % 2) + 1][:, :],
                                               scalar=b1[:, 2 + j, e:e + 1], in1=sil[:, u % 2, :],
                                               op0=ALU.add, op1=ALU.mult).then_inc(h_used, 1)
                    if e == 0:
                        dve.wait_ge(r_ps, c * 5 + 5)
                        V.tensor_tensor(xs, xs, bank[7][:, :].rearrange("p (t d) -> p t d", t=4),
                                        ALU.add).then_inc(r_dve, 1)
                    else:
                        weigh(e - 1)
                weigh(E - 1)

            dve.wait_ge(yw_used, NC * E + 2)
            with dve.Fori(0, NT) as t:
                V.bn_stats(stats[:, bass.ds(t, 1), :].rearrange("p a s -> p (a s)"),
                           x[:, bass.ds(t, 1), :].rearrange("p a d -> p (a d)"))
            link(V.memset(al[:, 3:4], 1.0))
            layer_norm(2)
            dve.wait_ge(g_const, 3)
            V.memset(bank[6][:, :], 0.0).then_inc(o_clear, 1)
            y_done = {}

            def layer1(w, kind, ahead, g, i):
                if kind == "X":
                    normalise(lambda t: bass.ds((w.batch + ahead) * TB + t, 1), i)
                    return
                if kind in "VTYF":
                    misc_full(dve, w)
                if kind in MISC:
                    misc, used = bank[MB[w.misc()]], m_used[w.misc()]
                if kind == "V":
                    lo, hi = i
                    V.tensor_tensor(vaug[:, lo:hi, :, 0:HD],
                                    misc[:, 0:(hi - lo) * D].rearrange("p (j h e) -> p j h e", h=NH, e=HD),
                                    bvb[:, :].rearrange("p (h e) -> p h e", h=NH).unsqueeze(1)
                                    .broadcast_to([P, hi - lo, NH, HD]), ALU.add).then_inc(used, 1)
                elif kind == "A":
                    u = w.before["A"]
                    t, r = divmod(i, 4)
                    dve.wait_ge(a_ps, w.no("A") + 1)
                    dve.sem_inc(apart, 1)
                    V.tensor_tensor_reduce(junk[:, u % 2, :], bank[u % 2][:, 0:KW], mask1[:, t, :], 1.0, -3.0e38,
                                           ALU.add, ALU.max, mx[:, g % 2, r, t:t + 1]).then_inc(a_used, 1)
                elif kind == "N":
                    top4 = mx[:, g % 2, :, 4 * i:4 * i + 4]
                    dve.wait_ge(a_used, w.no("A") + 2)
                    V.tensor_scalar(nmr[:, :, :], top4, -1.0, None, ALU.mult).then_inc(n_part, 1)
                    dve.wait_ge(n_part, w.no("N") + 1)
                    V.tensor_copy(nm[:, i, :, 0, :], nmr[:, :, :].bitcast(F32))
                    V.scalar_tensor_tensor(out=nm[:, i, :, 1, :], in0=top4, scalar=-1.0,
                                           in1=nmr[:, :, :].bitcast(F32), op0=ALU.mult,
                                           op1=ALU.subtract).then_inc(n_ready, 1)
                elif kind == "T":
                    sums = misc[:, :].rearrange("p (t r e) -> p t r e", t=4, r=4)
                    inv = rd[:, i, :].rearrange("p (t r e) -> p t r e", t=4, e=1)
                    V.reciprocal(inv, sums[:, :, :, HD:HD + 1]).then_inc(rd_ready, 1)
                    dve.wait_ge(rd_ready, w.no("T") + 1)
                    V.tensor_tensor(on[:, 4 * i:4 * i + 4, g * 32:(g + 1) * 32].rearrange("p t (r e) -> p t r e", r=4),
                                    sums[:, :, :, 0:HD], inv.broadcast_to([P, 4, 4, HD]), ALU.mult).then_inc(used, 1)
                elif kind == "Y":
                    xs = x[:, bass.ds(w.batch * TB + 4 * i, 4), :]
                    V.tensor_tensor(xs, xs, misc[:, :].rearrange("p (t d) -> p t d", t=4), ALU.add).then_inc(used, 1)
                    y_done[i] = (used, w.misc_fills() + 2)
                elif kind == "F":
                    dve.wait_ge(*y_done[i])
                    dve.wait_ge(out_done[i], w.batch * 16 + 16)
                    V.tensor_tensor(yo[:, i, :, :], x[:, bass.ds(w.batch * TB + 4 * i, 4), :],
                                    misc[:, :].rearrange("p (t d) -> p t d", t=4), ALU.add).then_inc(used, 1)

            Walk().run(dve, layer1)

        @block.tensor
        def _(pe):
            pe.sem_inc(xT_done, 2)
            pe.sem_inc(p_used, 8)

            def transposes(turn, g):
                pe.wait_ge(xn_ready, turn * 2 + g + 1)
                pe.wait_ge(xT_used, turn * 2 + g + 1)
                for t in range(4):
                    last = pe.transpose(bank[g][:, t * P:(t + 1) * P], xst[:, g, t, :], ident[:, :])
                last.then_inc(xT_done, 1)

            def mm(o, l, r_, first=True, last=True, **k):
                return pe.matmul(o, l, r_, start=first, stop=last, **k)

            pe.wait_ge(w_in, 16 * N_LOADS)
            cos, sin, nsin = (dft[:, k, :] for k in range(3))
            mm(bank[2][:, 0:R], w["Winv"][:, :], wb_t[:, 0:R])
            mm(bank[2][:, R:2 * R], w["Winv"][:, :], vb_t[:, 0:R])
            pe.transpose(bank[2][:, 2 * R:2 * R + D], w["WO"][:, :], ident[:, :])
            mm(bank[3][:, 0:D], wf[:, 0, :], cos, True, False)
            mm(bank[3][:, 0:D], wf[:, 1, :], sin, False, True)
            mm(bank[3][:, D:2 * D], wf[:, 1, :], cos, True, False)
            mm(bank[3][:, D:2 * D], wf[:, 0, :], nsin, False, True).then_inc(set1, 1)
            with pe.Fori(0, NC // 2) as i:
                for g in range(2):
                    transposes(i, g)
            pe.wait_ge(set1_sb, 1)
            pe.wait_ge(g_const, 2)
            mm(bank[4][:, 0:3 * R], w["WQ"][:, :], vb_t[:, :])
            mm(bank[4][:, 3 * R:6 * R], w["WK"][:, :], wb_t[:, :])
            mm(bank[4][:, 6 * R:8 * R], aT[:, 0, :], cos, True, False)
            mm(bank[4][:, 6 * R:8 * R], aT[:, 1, :], nsin, False, True)
            mm(bank[5][:, 0:D], ub2[:, :], woT[:, :])
            mm(bank[5][0:R, D:2 * D], ut[:, :], woT[:, :])
            mm(bank[5][0:1, 2 * D:3 * D], bb[:, 3:4], woT[:, :])
            for k in range(2):
                for g in range(HG):
                    last = mm(bank[5][:, 3 * D + k * HG + g:3 * D + k * HG + g + 1],
                              brep[0:1, k, 4 * g:4 * g + 4, :].rearrange("p h e -> p (h e)"), ones[0:1, 0:1])
            last.then_inc(set2, 1)
            pe.wait_ge(xT_used, NC + 2)
            for t in range(NT):
                last = mm(bank[0][:, t * E:(t + 1) * E], xnT[:, t * P:(t + 1) * P], Wr[:, :])
            last.then_inc(lg_ps, 1)
            pe.wait_ge(w9_ready, 1)
            for k in range(NC):
                if k >= 4:
                    pe.wait_ge(w9T_ready, k - 3)
                for t in range(4):
                    last = pe.transpose(bank[k % 4][0:E + 1, t * P:(t + 1) * P], w9[:, 4 * k + t, :], ident[:, :])
                last.then_inc(w9_ps, 1)

            pe.wait_ge(set2_sb, 1)
            pe.wait_ge(z_ready, B)
            pe.wait_ge(w9T_ready, NC)
            pe.wait_ge(w1_in, 16 * 4)
            with pe.Fori(0, NC) as c:
                xc, zc = xnT[:, bass.ds(c * C, C)], z[:, bass.ds(c * C, C)]

                def hidden(e):
                    for j in range(2):
                        u = 2 * e + j
                        pe.wait_ge(h_used, c * 2 * E + u + 1)
                        for half in range(2):
                            last = mm(bank[2 * (u % 2) + half][:, :], W1[:, e, half * HF + j * P:half * HF + (j + 1) * P], xc)
                        last.then_inc(h_ps, 1)

                def down(e):
                    pe.wait_ge(h_used, c * 2 * E + 2 * e + 4)
                    pe.wait_ge(y_used, c * E + e + 1)
                    for t in range(4):
                        for j in range(2):
                            last = mm(bank[4 + e % 2][:, t * P:(t + 1) * P], actT[:, e % 2, j, t * P:(t + 1) * P],
                                      W2[:, e, j, :], j == 0, j == 1)
                    last.then_inc(y_ps, 1)

                pe.wait_ge(r_act, c * 2 + 2)
                mm(bank[6][:, :], LQ[:, 0:2 * R], xc).then_inc(r_ps, 1)
                pe.wait_ge(r_dve, c * 4 + 4)
                mm(bank[7][:, :], LK[:, 0:2 * R], zc).then_inc(r_ps, 1)
                pe.wait_ge(r_act, c * 2 + 3)
                pe.sem_inc(apart, 1)
                mm(bank[6][0:R, :], LQ[:, 2 * R:3 * R], xc).then_inc(r_ps, 1)
                pe.wait_ge(r_dve, c * 4 + 5)
                mm(bank[7][:, :], LK[:, 2 * R:4 * R], zc).then_inc(r_ps, 1)
                hidden(0)
                pe.wait_ge(r_dve, c * 4 + 7)
                pe.wait_ge(w9c_ready, c + 1)
                for t in range(4):
                    s = slice(t * P, (t + 1) * P)
                    mm(bank[7][:, s], sB[:, s], UB[:, :], True, False)
                    mm(bank[7][:, s], tri[:, s], UT[:, :], False, False)
                    last = mm(bank[7][:, s], w9c[:, s], b2a[:, :], False, True)
                last.then_inc(r_ps, 1)
                for e in range(1, E):
                    hidden(e)
                    down(e - 1)
                down(E - 1)

            pe.wait_ge(identr_ready, 3)
            pe.wait_ge(h_used, NC * 2 * E + 2)
            pe.wait_ge(r_dve, NC * 4 + 4)
            pe.wait_ge(y_used, NC * E + 2)
            pe.wait_ge(o_clear, 1)
            pending = []

            def layer1(w, kind, ahead, g, i):
                tiles = [slice(k * P, (k + 1) * P) for k in range(4)]
                if kind in MISC:
                    pe.wait_ge(m_used[w.misc()], w.misc_fills() + 1)
                    o = bank[MB[w.misc()]]
                if kind in "VKF":
                    for bank_of, fills in pending:
                        if bank_of != w.misc():
                            pe.wait_ge(m_used[bank_of], fills)
                    pending.clear()
                if kind == "X":
                    pe.wait_ge(xn_ready, w.no("X") + NC + 1)
                    for k in range(4):
                        last = pe.transpose(o[:, tiles[k]], xst[:, i, k, :], ident[:, :])
                    last.then_inc(m_ps, 1)
                    pending.append((w.misc(), w.misc_fills() + 2))
                elif kind == "V":
                    for k, j in enumerate(range(*i)):
                        rows = xn2T[:, ST - 1 + C * j:C * (j + 1):ST] if j < 2 else xn2T[:, (j - 2) * P:(j - 1) * P]
                        last = mm(o[:, tiles[k]], rows, cw[:, 2 * D:3 * D])
                    last.then_inc(m_ps, 1)
                elif kind == "K":
                    mm(o[:, :], wrep[:, i // 2, 4 * g:4 * g + 4, :].rearrange("p h e -> p (h e)"),
                       xn2T[:, (i % 2) * C:(i % 2 + 1) * C]).then_inc(m_ps, 1)
                elif kind == "A":
                    u = w.before["A"]
                    t, r = divmod(i, 4)
                    if i == 0:
                        pe.wait_ge(qk_ready, w.no("K") + 2)
                        pe.wait_ge(q_rows, w.no("K", 4) * 64 + 64)
                    pe.wait_ge(a_used, w.no("A") + 1)
                    q = qz[:, g % 2, r, t * P:(t + 1) * P]
                    mm(bank[u % 2][:, 0:NS], q, ks[:, g % 2, ST - 1:T:ST])
                    mm(bank[u % 2][:, NS:KW], q, ks[:, g % 2, t * P:(t + 1) * P]).then_inc(a_ps, 1)
                elif kind == "M":
                    pe.wait_ge(n_ready, w.no("N"))
                    pe.sem_inc(apart, 1)
                    pe.transpose(o[0:4 * TB, 0:P], nm[:, i, :, :, :].rearrange("p r s t -> p (r s t)"),
                                 ident[:, :]).then_inc(m_ps, 1)
                elif kind == "S":
                    u = w.before["S"]
                    qc, r, part = i // 12, i % 4, PARTS[i % 12 // 4]
                    if i % 12 == 0:
                        pe.wait_ge(m_rows, w.no("M") * 128 + 128)
                    pe.wait_ge(p_ready, w.no("S") + 1)
                    o = bank[3 + u % 3]
                    q = qz[:, g % 2, r, qc * C:(qc + 1) * C]
                    if part < 2:
                        keys = ks[:, g % 2, ST - 1 + C * part:C * (part + 1):ST]
                        last = mm(o[:, :], keys, q, True, part != qc)
                        if part == qc:
                            last = mm(o[:, :], identr[:, :], mstr_r[:, :], False, True)
                    else:
                        for j, s in enumerate(tiles):
                            mm(o[:, s], ks[:, g % 2, qc * C + j * P:qc * C + (j + 1) * P], q[:, s],
                               j == 0, False, skip_group_check=True)
                        last = mm(o[:, :].rearrange("p (t k) -> p t k", t=4), identr[:, :],
                                  mloc_r[:, :].unsqueeze(1).broadcast_to([P, 4, P]), False, True,
                                  skip_group_check=True)
                    last.then_inc(s_ps, 1)
                elif kind == "P":
                    u = w.before["P"]
                    qc, r, part = i // 12, i % 4, PARTS[i % 12 // 4]
                    pe.wait_ge(p_ready, w.no("P") + 4)
                    if i % 12 == 0:
                        pe.wait_ge(on_ready, w.no("O") + 1)
                    o = bank[6][32 * r:32 * r + HD + 1, :]
                    if part < 2:
                        last = mm(o, vaug[:, part, 4 * g + r, :], pT[:, u % 8, :], False, part == 1,
                                  skip_group_check=True)
                    else:
                        for j, s in enumerate(tiles):
                            last = mm(o[:, s], vaug[:, 2 + 4 * qc + j, 4 * g + r, :], pT[:, u % 8, s],
                                      j == 0, False, skip_group_check=True)
                    last.then_inc(p_used, 1)
                elif kind == "T":
                    pe.wait_ge(on_ready, w.no("O") + 1)
                    for s in tiles:
                        last = pe.transpose(o[:, s], onum[:, i, s], ident[:, :])
                    last.then_inc(m_ps, 1)
                    attended[i] = (w.misc(), w.misc_fills() + 2)
                elif kind == "U":
                    bank_of, fills = attended[i]
                    if bank_of != w.misc():
                        pe.wait_ge(m_used[bank_of], fills)
                    for k, s in enumerate(tiles):
                        last = pe.transpose(o[:, s], on[:, 4 * i + k, :], ident[:, :])
                    last.then_inc(m_ps, 1)
                    pending.append((w.misc(), w.misc_fills() + 2))
                elif kind == "Y":
                    for k, s in enumerate(tiles):
                        mm(o[:, s], xn2T[:, i * C + k * P:i * C + (k + 1) * P], G[:, :], True, False)
                        last = mm(o[:, s], ones[0:2, 0:P], bias2[:, :], False, True)
                    last.then_inc(m_ps, 1)
                elif kind == "F":
                    for k, s in enumerate(tiles):
                        last = mm(o[:, s], oT[:, i, s], cproj[:, :])
                    last.then_inc(m_ps, 1)

            attended = {}
            Walk().run(pe, layer1)


INS = """L0_attn_x L0_attn_WQ L0_attn_WK L0_attn_WO L0_attn_Winv L0_attn_U_b L0_attn_V_b L0_attn_W_b L0_attn_bias_b
         L0_attn_U_t L0_attn_V_t L0_attn_W_t L0_attn_X_t L0_attn_bias_t L0_attn_alpha_bi L0_attn_alpha_tri
         L0_ffn_W1 L0_ffn_b1 L0_ffn_W2 L0_ffn_b2 L0_ffn_Wr L0_ffn_br
         L1_attn_c_attn_w L1_attn_c_attn_b L1_attn_c_proj_w L1_attn_c_proj_b L1_ffn_w_freq_real L1_ffn_w_freq_imag L1_ffn_bias""".split()


def constants():
    k = np.arange(D)
    angle = 2.0 * np.pi * ((k[:, None] * k[None, :]) % D) / D
    low = np.zeros((P, 2))
    low[:, 0] = k % 32 // HD == 2
    low[:, 1] = k % 32 // HD == 1
    made = {"dft": np.stack([np.cos(angle), np.sin(angle), -np.sin(angle)], 1), "low_rows": low,
            "rcount": 1.0 / np.arange(1, T + 1), "desc": np.arange(E, 0, -1), "ident": np.eye(P)}
    return {n: np.ascontiguousarray(v, np.float32) for n, v in made.items()}


def kernel(**inputs):
    import concourse.bacc as bacc
    from concourse.bass_utils import run_bass_kernel_spmd

    nc = bacc.Bacc("TRN2", target_bir_lowering=False, num_devices=1)
    arrays, args = {}, {}
    for name in INS:
        v = np.asarray(inputs[name])
        if name == "L0_ffn_b1":
            v = v.reshape(E, 2 * HF // P, P).transpose(2, 1, 0)
        arrays[name + "_dram"] = np.ascontiguousarray(v.reshape(v.shape or (1,)))
    for name, v in constants().items():
        arrays[name + "_dram"] = v
    for name, v in arrays.items():
        args[name[:-5]] = nc.dram_tensor(name, v.shape, mybir.dt.from_np(v.dtype), kind="ExternalInput").ap()
    out = nc.dram_tensor("out_dram", (B, T, D), F32, kind="ExternalOutput").ap()
    build(nc, args, out)
    got = run_bass_kernel_spmd(nc, [arrays], core_ids=[0])
    return got.results[0]["out_dram"]
```

```python
from contextlib import ExitStack

import numpy as np

import concourse.bass as bass
from concourse import mybir

F32 = mybir.dt.float32
F32R = mybir.dt.float32r
ALU = mybir.AluOpType
ACT = mybir.ActivationFunctionType
AX = mybir.AxisListType

B, T, D, R = 4, 1024, 128, 64
P = 128
NT = B * T // P
TB = T // P
C = 512
NC = B * T // C
E, HF = 8, 256
NH, HD = 16, 8
HG = 4
ST = 4
NS = T // ST
KW = NS + P
MASK = -10000.0
FAR = -1.0e38
EPS = 1e-5
KQ = 3 * HD
KM = KQ + 2

WEIGHTS = ["WQ", "WK", "WO", "Winv"]


class Chain:

    def __init__(self, eng, sem):
        self.eng, self.sem, self.n = eng, sem, 0

    def __call__(self, ins):
        self.n += 1
        ins.then_inc(self.sem, 1)
        self.eng.wait_ge(self.sem, self.n)


MISC = "XVKMYTUF"
MB = (2, 7)
AB = (0, 1, 5)
SB = (3, 4)
A_AT = 5.0
N_LOADS = 28
PARTS = (2, 0, 1)


def layer1_steps():
    group, cut = 24, 12
    batch = HG * group
    timed = []

    def at(time, kind, b, g, item):
        timed.append((time, len(timed), (kind, b, g, item)))

    for b in range(B):
        for i in range(2):
            at(batch * b - 37 + 3 * i, "L", b, 0, i)
            at(batch * b - 33.5 + 3 * i, "X", b, 0, i)
            at(batch * b + 56 + 3 * i, "Y", b, 0, i)
            at(batch * b + 92 + 12 * i, "U", b, 0, i)
            at(batch * b + 94 + 12 * i, "F", b, 0, i)
        for i, tiles in enumerate(((0, 3), (3, 6), (6, 8), (8, 10))):
            at(batch * b - 20 + 3 * i, "V", b, 0, tiles)
        at(batch * b + 1.6, "C", b, 0, 0)
        for g in range(HG):
            now = batch * b + group * g
            for i, early in enumerate((-3.0, -2.0, 0.2, 1.2)):
                at(now - group + early, "K", b, g, i)
            at(now - group + 0.1, "Q", b, g, 0)
            for i in range(32):
                at(now - group + A_AT + i * 0.75, "A", b, g, i)
            for half in range(2):
                at(now - group + A_AT + 11.9 + 12 * half, "N", b, g, half)
                at(now - group + A_AT + 13.9 + 12 * half, "M", b, g, half)
                at(now + 14 + 12 * half, "O", b, g, half)
                at(now + 16.2 + 12 * half, "T", b, g, half)
            for i in range(24):
                at(now + i, "S", b, g, i)
                at(now + i // 4 * 4 + 5.5, "P", b, g, i)

    def between(start, end, b):
        return [(k, sb - b, g, item) for t, _, (k, sb, g, item) in sorted(timed) if start <= t < end]

    far = 1000 * B
    turns = [between(batch * b + cut, batch * (b + 1) + cut, b) for b in range(B - 1)]
    assert all(t == turns[0] for t in turns)
    return between(-far, cut, 0), turns[0], between(batch * (B - 1) + cut, far, B - 1)


class Walk:

    def __init__(self):
        self.before, self.per = dict.fromkeys(KINDS, 0), dict.fromkeys(KINDS, 0)
        self.turn = 0
        self.batch = 0

    def no(self, kind, of=1):
        assert self.per[kind] % of == 0 and self.before[kind] % of == 0
        return self.turn * (self.per[kind] // of) + self.before[kind] // of

    def misc(self):
        return sum(self.before[k] for k in MISC) % 2

    def misc_no(self):
        return self.turn * sum(self.per[k] for k in MISC) + sum(self.before[k] for k in MISC)

    def misc_fills(self):
        return self.turn * (sum(self.per[k] for k in MISC) // 2) + sum(self.before[k] for k in MISC) // 2

    def take(self, steps, do):
        for step in steps:
            do(self, *step)
            self.before[step[0]] += 1

    def run(self, eng, do):
        first, turn, last = layer1_steps()
        self.take(first, do)
        start, per = dict(self.before), {k: sum(s[0] == k for s in turn) for k in KINDS}
        assert sum(start[k] for k in MISC) % 2 == 0 and sum(per[k] for k in MISC) % 2 == 0
        with eng.Fori(0, B - 1) as b:
            self.turn, self.batch, self.per = b, b, per
            self.take(turn, do)
        self.turn, self.batch = 0, B - 1
        self.before = {k: start[k] + (B - 1) * per[k] for k in KINDS}
        self.take(last, do)


KINDS = "LXVCKQANMSPOTUYF"


def build(nc, a, out):
    x_d = a["L0_attn_x"].rearrange("b (t p) d -> p (b t) d", p=P)
    out_d = out.rearrange("b (t p) d -> b p t d", p=P)
    with ExitStack() as ctx:
        def sb(name, shape, dt=F32, scope=ctx):
            return scope.enter_context(nc.sbuf_tensor(name, shape, dt))

        def sem(name):
            return ctx.enter_context(nc.semaphore(name))

        bank = [ctx.enter_context(nc.psum_tensor(f"bank{i}", [P, C], F32)) for i in range(8)]

        x = sb("x_tok", [P, NT, D])
        tokens_a = sb("tokens_a", [P, 2 * B * T])
        weights_a = sb("weights_a", [P, 3 * E * 2 * D])
        routing_a = sb("routing_a", [P, B * T])
        xnT = tokens_a[:, 0:B * T]
        z = tokens_a[:, B * T:2 * B * T]
        xst = sb("xst", [P, 2, 4, D])
        stats = sb("stats", [P, NT, 6])
        ln = sb("ln", [P, 10, NT])
        ident = sb("ident", [P, P])
        identr = sb("identr", [P, P], F32R)
        ones = sb("ones", [P, T])
        al = sb("al", [P, 4])
        bb = sb("bb", [P, 4])
        G = sb("G", [P, D])
        W1 = weights_a[:, 0:E * 2 * HF].rearrange("p (e h) -> p e h", e=E)
        b1 = sb("b1", [P, 2 * HF // P, E])
        W2 = weights_a[:, E * 2 * HF:E * 3 * HF].rearrange("p (e k d) -> p e k d", e=E, k=2)
        b2a = sb("b2a", [E + 1, D])
        Wr = sb("Wr", [P, E])
        brb = sb("brb", [P, E])
        gs = sb("gs", [P, 4, NT])
        desc = sb("desc", [P, E])
        w9 = sb("w9", [P, NT, E + 1])
        w9T = routing_a[0:E + 1, :]
        cw = sb("cw", [P, 3 * D])
        cb = sb("cb", [1, 3 * D])
        wrep = sb("wrep", [P, 2, NH, 32])
        brep = sb("brep", [1, 2, NH, 32])
        bqk = sb("bqk", [P, 2, HG])
        bqk_low = sb("bqk_low", [P, 2, HG])
        lowm = sb("lowm", [P, 2])
        bvb = sb("bvb", [P, D])
        cproj = sb("cproj", [P, D])
        bias2 = sb("bias2", [2, D])
        mask1 = routing_a[:, 0:TB * KW].rearrange("p (t k) -> p t k", t=TB)
        mstr = sb("mstr", [P, C])
        mloc = sb("mloc", [P, P])
        mstr_r = sb("mstr_r", [P, C], F32R)
        mloc_r = sb("mloc_r", [P, P], F32R)
        maskc = sb("maskc", [P, 2])
        NV = (2 + TB) * NH * (HD + 1)
        vaug = tokens_a[:, 0:NV].rearrange("p (j h e) -> p j h e", h=NH, e=HD + 1)
        rd = sb("rd", [P, 2, 16])
        mx = sb("mx", [P, 2, 4, TB])
        nm = sb("nm", [P, 2, 4, 2, TB // 2])
        nmr = sb("nmr", [P, 4, TB // 2], F32R)
        mT = sb("mT", [4 * TB, 2, P], F32R)
        vnext = tokens_a[:, NV:2 * NV].rearrange("p (j h e) -> p j h e", h=NH, e=HD + 1)
        pT = tokens_a[:, 2 * NV:2 * NV + 8 * C].rearrange("p (u q) -> p u q", u=8)
        onum = tokens_a[:, 2 * NV + 8 * C:2 * NV + 10 * C].rearrange("p (u q) -> p u q", u=2)
        on = weights_a[:, 0:TB * D].rearrange("p (t d) -> p t d", t=TB)
        oT = weights_a[:, TB * D:TB * D + T].rearrange("p (u q) -> p u q", u=2)
        yo = weights_a[:, 2 * T:2 * T + 2 * C].rearrange("p (u t d) -> p u t d", u=2, t=4)
        layer0 = ExitStack()
        W1h = sb("W1h", [P, E, 2 * HF], F32R, scope=layer0)
        W1l = sb("W1l", [P, E, 2 * HF], F32R, scope=layer0)
        rcount = sb("rcount", [P, T], scope=layer0)
        w = {n: sb("w_" + n, [P, D], scope=layer0) for n in WEIGHTS}
        vb_t = sb("rq", [P, 3 * R], scope=layer0)
        wb_t = sb("rk", [P, 3 * R], scope=layer0)
        ub2 = sb("ub2", [P, 2 * R], scope=layer0)
        ut = sb("ut", [P, R], scope=layer0)
        LQ = sb("LQ", [P, 3 * R], scope=layer0)
        LK = sb("LK", [P, 4 * R], scope=layer0)
        UB = sb("UB", [P, D], scope=layer0)
        UT = sb("UT", [R, D], scope=layer0)
        woT = sb("woT", [P, D], scope=layer0)
        dft = sb("dft", [P, 3, D], scope=layer0)
        wf = sb("wf", [P, 2, D], scope=layer0)
        aT = sb("aT", [P, 2, D], scope=layer0)
        lg = sb("lg", [P, NT, E], scope=layer0)
        gt = sb("gt", [P, 4, NT, E], scope=layer0)
        w9c = sb("w9c", [E + 1, C], scope=layer0)
        xh = sb("xh", [P, C], F32R, scope=layer0)
        xl = sb("xl", [P, C], F32R, scope=layer0)
        sa = sb("sa", [P, C], scope=layer0)
        sB = sb("sB", [P, C], scope=layer0)
        sc = sb("sc", [R, C], scope=layer0)
        tc = sb("tc", [R, C], scope=layer0)
        tri = sb("tri", [R, C], scope=layer0)
        sil = sb("sil", [P, 2, C], scope=layer0)
        actT = sb("actT", [P, 2, 2, C], scope=layer0)
        yw = sb("yw", [P, 2, 4, D], scope=layer0)
        layer0.close()
        qz = sb("qz", [P, 2, 4, T], F32R)
        xn2T = sb("xn2T", [P, T])
        xn2h = sb("xn2h", [P, T], F32R)
        xn2l = sb("xn2l", [P, T], F32R)
        wreph = sb("wreph", [P, 2, NH, 32], F32R)
        wrepl = sb("wrepl", [P, 2, NH, 32], F32R)
        kt = sb("kt", [P, 2, C])
        junk = sb("junk", [P, len(AB), KW])
        hp = sb("hp", [P, 2, C], F32R)
        qs = sb("qs", [P, T], F32R)
        ks = sb("ks", [P, 2, T], F32R)

        x_in = [sem(f"x_in{b}") for b in range(B)]
        early_in, w_in, w1_in = sem("early_in"), sem("w_in"), sem("w1_in")
        g_const, identr_ready = sem("g_const"), sem("identr_ready")
        g_chain, d_chain = sem("g_chain"), sem("d_chain")
        var_ready, sq_ready = sem("var_ready"), sem("sq_ready")
        xn_ready, xT_done, xT_used = sem("xn_ready"), sem("xT_done"), sem("xT_used")
        z_sum, z_ready = sem("z_sum"), sem("z_ready")
        set1, set1_sb, set2, set2_sb = sem("set1"), sem("set1_sb"), sem("set2"), sem("set2_sb")
        lg_ps, dif_ready, exp_ready, w9_ready = sem("lg_ps"), sem("dif_ready"), sem("exp_ready"), sem("w9_ready")
        w9_ps, w9T_ready, w9c_ready = sem("w9_ps"), sem("w9T_ready"), sem("w9c_ready")
        r_ps, r_act, r_dve = sem("r_ps"), sem("r_act"), sem("r_dve")
        w1h_ready, w1l_ready, xh_ready, xl_ready = sem("w1h_ready"), sem("w1l_ready"), sem("xh_ready"), sem("xl_ready")
        h_ps, sil_ready, h_used = sem("h_ps"), sem("sil_ready"), sem("h_used")
        y_ps, y_used, yw_used = sem("y_ps"), sem("y_used"), sem("yw_used")
        m_ps, m_used = sem("m_ps"), [sem("m_used0"), sem("m_used1")]
        wreph_ready, wrepl_ready, xn2l_ready = sem("wreph_ready"), sem("wrepl_ready"), sem("xn2l_ready")
        qk_ready, q_rows, qz_clear = sem("qk_ready"), sem("q_rows"), sem("qz_clear")
        a_ps, a_used = sem("a_ps"), sem("a_used")
        n_part, n_ready, m_rows = sem("n_part"), sem("n_ready"), sem("m_rows")
        v_ready, s_ps, p_ready, p_used = sem("v_ready"), sem("s_ps"), sem("p_ready"), sem("p_used")
        on_ready, rd_ready, o_clear = sem("on_ready"), sem("rd_ready"), sem("o_clear")
        apart = sem("apart")
        out_done = [sem(f"out_done{i}") for i in range(2)]

        block = ctx.enter_context(nc.Block())

        def misc_full(eng, w):
            eng.wait_ge(m_ps, w.misc_no() + 1)

        def misc_read(eng, w):
            eng.wait_ge(m_used[w.misc()], w.misc_fills() + 2)

        @block.sync
        def _(sp):
            for b in range(B):
                sp.dma_start(x[:, b * TB:(b + 1) * TB, :], x_d[:, b * TB:(b + 1) * TB, :]).then_inc(x_in[b], 16)
            loads = [(w[k][:, :], a["L0_attn_" + k]) for k in WEIGHTS]
            loads += [(vb_t[:, 0:R], a["L0_attn_V_b"]), (vb_t[:, 2 * R:3 * R], a["L0_attn_V_t"]),
                      (wb_t[:, 0:R], a["L0_attn_W_b"]), (wb_t[:, 2 * R:3 * R], a["L0_attn_W_t"]),
                      (ub2[:, 0:R], a["L0_attn_U_b"]), (ub2[:, R:2 * R], a["L0_attn_U_b"]),
                      (ut[:, :], a["L0_attn_U_t"]), (LK[:, 3 * R:4 * R], a["L0_attn_X_t"]),
                      (al[:, 0:1], a["L0_attn_alpha_bi"].partition_broadcast(P)),
                      (al[:, 1:2], a["L0_attn_alpha_tri"].partition_broadcast(P)),
                      (bb[:, 0:1], a["L0_attn_bias_b"].rearrange("(p a) -> p a", a=1)),
                      (bb[:, 1:2], a["L0_attn_bias_t"].rearrange("(p a) -> p a", a=1)),
                      (dft[:, :, :], a["dft"]), (wf[:, 0, :], a["L1_ffn_w_freq_real"]),
                      (wf[:, 1, :], a["L1_ffn_w_freq_imag"]), (b2a[1:E + 1, :], a["L0_ffn_b2"]),
                      (cw[:, :], a["L1_attn_c_attn_w"]),
                      (cb[:, :], a["L1_attn_c_attn_b"].rearrange("(a n) -> a n", a=1)),
                      (bvb[:, :], a["L1_attn_c_attn_b"][2 * D:3 * D].partition_broadcast(P)),
                      (lowm[:, :], a["low_rows"]), (rcount[:, :], a["rcount"].partition_broadcast(P)),
                      (cproj[:, :], a["L1_attn_c_proj_w"]),
                      (bias2[0:1, :], a["L1_attn_c_proj_b"].rearrange("(a n) -> a n", a=1)),
                      (bias2[1:2, :], a["L1_ffn_bias"].rearrange("(a n) -> a n", a=1))]
            assert len(loads) == N_LOADS
            for dst, src in loads:
                sp.dma_start(dst, src).then_inc(w_in, 16)
            sp.dma_start(W1[:, :, :], a["L0_ffn_W1"].rearrange("e d h -> d e h")).then_inc(w1_in, 16)
            for k in range(2):
                sp.dma_start(W2[:, :, k, :], a["L0_ffn_W2"][:, k * P:(k + 1) * P, :].rearrange("e p d -> p e d")).then_inc(w1_in, 16)
            sp.dma_start(b1[:, :, :], a["L0_ffn_b1"]).then_inc(w1_in, 16)

            def layer1(w, kind, ahead, g, i):
                if kind == "Q":
                    sp.wait_ge(qk_ready, w.no("K") + 2)
                    sp.sem_inc(apart, 1)
                    sp.wait_ge(p_ready, w.no("S") + len(SB))
                    for r in range(4):
                        rows = slice(32 * r, 32 * r + 32)
                        sp.dma_start(qz[rows, g % 2, r, :].bitcast(F32), qs[rows, :].bitcast(F32)).then_inc(q_rows, 16)
                elif kind == "M":
                    misc_read(sp, w)
                    for r in range(4):
                        to = qz[32 * r + KQ:32 * r + KM, g % 2, r, i * C:(i + 1) * C].rearrange("s (t q) -> s t q", t=4)
                        sp.dma_start(to.bitcast(F32), mT[8 * r:8 * r + 8, i, :].bitcast(F32)).then_inc(m_rows, 16)
                elif kind == "F":
                    misc_read(sp, w)
                    sp.dma_start(out_d[bass.ds(w.batch, 1), :, 4 * i:4 * i + 4, :].rearrange("a p t d -> (a p) t d"),
                                 yo[:, i, :, :]).then_inc(out_done[i], 16)

            sp.wait_ge(qz_clear, 8)
            Walk().run(sp, layer1)
            for k in range(2):
                sp.wait_ge(out_done[k], 16 * (B + 1))

        @block.scalar
        def _(act):
            act.sem_inc(r_act, 2)
            act.sem_inc(xT_used, 2)
            act.sem_inc(out_done[0], 16)
            act.sem_inc(out_done[1], 16)
            act.sem_inc(p_ready, len(SB))
            act.sem_inc(on_ready, 1)
            act.sem_inc(v_ready, 1)
            for dst, src in ((ident[:, :], a["ident"]), (Wr[:, :], a["L0_ffn_Wr"]),
                             (brb[:, :], a["L0_ffn_br"].partition_broadcast(P)),
                             (desc[:, :], a["desc"].partition_broadcast(P))):
                act.dma_start(dst, src).then_inc(early_in, 16)

            def root(n):
                act.wait_ge(var_ready, n)
                nc.scalar.activation(ln[:, 2, :], ln[:, 1, :], ACT.Sqrt).then_inc(sq_ready, 1)

            def xT_out(dst, turn, g):
                act.wait_ge(xT_done, turn * 2 + g + 3)
                nc.scalar.activation(dst, bank[g][:, :], ACT.Copy).then_inc(xT_used, 1)

            root(1)
            with act.Fori(0, NC // 2) as i:
                for g in range(2):
                    xT_out(xnT[:, bass.ds(i * 2 * C + g * C, C)], i, g)
            act.wait_ge(early_in, 16 * 4)
            nc.scalar.activation(identr[:, :], ident[:, :], ACT.Copy).then_inc(identr_ready, 1)
            act.wait_ge(g_const, 1)
            nc.scalar.activation(mstr_r[:, :], mstr[:, :], ACT.Copy).then_inc(identr_ready, 1)
            nc.scalar.activation(mloc_r[:, :], mloc[:, :], ACT.Copy).then_inc(identr_ready, 1)
            act.wait_ge(w1_in, 16 * 4)
            for e in range(E):
                nc.scalar.activation(W1h[:, e, :], W1[:, e, :], ACT.Copy).then_inc(w1h_ready, 1)
            act.wait_ge(dif_ready, 1)
            nc.scalar.activation(gs[:, 3, :], gs[:, 2, :], ACT.Exp).then_inc(exp_ready, 1)
            for k in range(NC):
                act.wait_ge(w9_ps, k + 1)
                nc.scalar.activation(w9T[:, k * C:(k + 1) * C], bank[k % 4][0:E + 1, :], ACT.Copy).then_inc(w9T_ready, 1)

            with act.Fori(0, NC) as c:
                nc.scalar.activation(xh[:, :], xnT[:, bass.ds(c * C, C)], ACT.Copy).then_inc(xh_ready, 1)
                act.wait_ge(r_ps, c * 5 + 1)
                act.wait_ge(r_dve, c * 4 + 1)
                nc.scalar.activation(sa[:, :], bank[6][:, :], ACT.Copy).then_inc(r_act, 1)
                act.wait_ge(r_ps, c * 5 + 3)
                act.wait_ge(r_dve, c * 4 + 2)
                nc.scalar.activation(sc[:, :], bank[6][0:R, :], ACT.Copy).then_inc(r_act, 1)
                for e in range(E):
                    for j in range(2):
                        u = 2 * e + j
                        act.wait_ge(h_ps, c * 2 * E + u + 1)
                        act.wait_ge(h_used, c * 2 * E + u + 1)
                        nc.scalar.activation(sil[:, u % 2, :], bank[2 * (u % 2)][:, :], ACT.Silu,
                                             bias=b1[:, j, e:e + 1]).then_inc(sil_ready, 1)

            def clear_qz(g):
                for r in range(4):
                    nc.scalar.activation(qz[:, g, r, :], ones[:, :], ACT.Copy, scale=0.0).then_inc(qz_clear, 1)

            clear_qz(0)
            act.wait_ge(yw_used, NC * E + 2)
            nc.scalar.activation(wreph[:, :, :, :], wrep[:, :, :, :], ACT.Copy).then_inc(wreph_ready, 1)
            root(2)
            clear_qz(1)

            def layer1(w, kind, ahead, g, i):
                if kind in "XU":
                    misc_full(act, w)
                    dst = xn2T[:, i * C:(i + 1) * C] if kind == "X" else oT[:, i, :]
                    if kind == "X":
                        nc.scalar.activation(xn2h[:, i * C:(i + 1) * C], bank[MB[w.misc()]][:, :], ACT.Copy)
                    nc.scalar.activation(dst, bank[MB[w.misc()]][:, :], ACT.Copy).then_inc(m_used[w.misc()], 1)
                elif kind == "K":
                    misc_full(act, w)
                    act.wait_ge(qk_ready, w.no("K") + 1)
                    n, k = w.before["K"] % 2, i // 2
                    nc.scalar.activation(hp[:, n, :], bank[MB[w.misc()]][:, :], ACT.Identity,
                                         bias=bqk_low[:, k, g:g + 1], scale=lowm[:, k:k + 1])
                    nc.scalar.activation(kt[:, n, :], bank[MB[w.misc()]][:, :], ACT.Identity,
                                         bias=bqk[:, k, g:g + 1]).then_inc(m_used[w.misc()], 1)
                elif kind == "M":
                    misc_full(act, w)
                    act.wait_ge(m_rows, w.no("M") * 64 + 64)
                    nc.scalar.activation(mT[:, i, :], bank[MB[w.misc()]][0:4 * TB, 0:P],
                                         ACT.Copy).then_inc(m_used[w.misc()], 1)
                elif kind == "S":
                    u = w.before["S"]
                    act.wait_ge(s_ps, w.no("S") + 1)
                    act.wait_ge(p_used, w.no("S") + 1)
                    later = (PARTS[i % 12 // 4], i // 12) == (1, 0)
                    nc.scalar.activation(pT[:, u % 8, :], bank[SB[u % len(SB)]][:, :], ACT.Exp,
                                         bias=maskc[:, 0:1] if later else 0.0).then_inc(p_ready, 1)
                elif kind == "V":
                    values[w.misc()] = w.misc_fills() + 2
                elif kind == "C":
                    for bank_of, fills in values.items():
                        act.wait_ge(m_used[bank_of], fills)
                    act.wait_ge(p_used, w.no("P") + 8)
                    nc.scalar.activation(vaug[:, :, :, :], vnext[:, :, :, :], ACT.Copy).then_inc(v_ready, 1)
                elif kind == "O":
                    act.wait_ge(p_used, w.no("P") + 8)
                    nc.scalar.activation(onum[:, i, :], bank[6][:, :], ACT.Copy).then_inc(on_ready, 1)

            values = {}
            Walk().run(act, layer1)

        @block.gpsimd
        def _(pool):
            pool.sem_inc(yw_used, 2)
            pool.sem_inc(qk_ready, 2)
            pool.sem_inc(m_rows, 64)
            pool.sem_inc(q_rows, 64)
            link = Chain(pool, g_chain)
            nc.gpsimd.memset(ones[:, :], 1.0)
            nc.gpsimd.memset(maskc[:, :], MASK)
            nc.gpsimd.memset(w9[:, :, 0:1], 1.0)
            nc.gpsimd.memset(mstr[:, :], 0.0)
            link(nc.gpsimd.memset(mloc[:, :], 0.0))
            nc.gpsimd.memset(wrep[:, :, :, :], 0.0)
            nc.gpsimd.memset(brep[:, :, :, :], 0.0)
            nc.gpsimd.affine_select(out=mstr[:, :], in_=mstr[:, :], compare_op=ALU.is_ge, fill=MASK,
                                    base=-(ST - 1), pattern=[[1, C]], channel_multiplier=-ST)
            link(nc.gpsimd.affine_select(out=mloc[:, :], in_=mloc[:, :], compare_op=ALU.is_ge, fill=MASK,
                                         base=0, pattern=[[1, P]], channel_multiplier=-1))
            for lo, other in ((0, 64), (64, 0)):
                last = nc.gpsimd.memset(mloc[lo:lo + 64, other:other + 64], FAR)
            link(last)
            link(nc.gpsimd.memset(brep[:, 1, :, KQ:KM], 1.0))
            pool.sem_inc(g_const, 1)
            pool.wait_ge(w_in, 16 * N_LOADS)
            scale = float(np.float32(1) / np.sqrt(np.float32(HD)))
            for src, dst in ((cw, wrep), (cb, brep)):
                for s in range(3):
                    for k in range(2):
                        last = nc.gpsimd.tensor_scalar(dst[:, k, :, s * HD:(s + 1) * HD],
                                                       src[:, k * D:(k + 1) * D].rearrange("p (h e) -> p h e", h=NH),
                                                       scale if k == 0 else 1.0, None, ALU.mult)
            last.then_inc(g_const, 1)
            for b in range(B):
                pool.wait_ge(z_sum, b + 1)
                nc.gpsimd.tensor_tensor(z[:, b * T:(b + 1) * T], z[:, b * T:(b + 1) * T], rcount[:, :],
                                        ALU.mult).then_inc(z_ready, 1)
            for e in range(E):
                pool.wait_ge(w1h_ready, e + 1)
                nc.gpsimd.tensor_tensor(W1l[:, e, :], W1[:, e, :], W1h[:, e, :].bitcast(F32),
                                        ALU.subtract).then_inc(w1l_ready, 1)
            pool.wait_ge(w9T_ready, NC)

            def layer0(c, between):
                pool.wait_ge(r_dve, c * 4 + 4)
                nc.gpsimd.tensor_copy(w9c[:, :], w9T[:, bass.ds(c * C, C)]).then_inc(w9c_ready, 1)
                pool.wait_ge(r_dve, c * 4 + 8)
                for e in range(E):
                    pool.wait_ge(y_used, c * E + e + 3)
                    pool.wait_ge(yw_used, c * E + e + 2)
                    pool.sem_inc(apart, 1)
                    xs = x[:, bass.ds(c * 4, 4), :]
                    nc.gpsimd.tensor_tensor(xs, xs, yw[:, e % 2, :, :], ALU.add).then_inc(yw_used, 1)
                    if 1 <= e <= len(between):
                        pool.wait_ge(yw_used, c * E + e + 3)
                        between[e - 1]()

            with pool.Fori(0, NC - 1) as c:
                layer0(c, [])

            def clear_mask():
                nc.gpsimd.memset(vnext[:, :, :, HD:HD + 1], 1.0)
                link(nc.gpsimd.memset(mask1, 0.0))

            def mask_global():
                link(nc.gpsimd.affine_select(out=mask1[:, :, 0:NS], in_=mask1[:, :, 0:NS], compare_op=ALU.is_ge,
                                             fill=MASK, base=-(ST - 1), pattern=[[P, TB], [-ST, NS]],
                                             channel_multiplier=1))

            def mask_local():
                link(nc.gpsimd.affine_select(out=mask1[:, :, NS:KW], in_=mask1[:, :, NS:KW], compare_op=ALU.is_ge,
                                             fill=MASK, base=0, pattern=[[0, TB], [-1, P]], channel_multiplier=1))

            def mask_far():
                for lo, other in ((0, 64), (64, 0)):
                    last = nc.gpsimd.memset(mask1[lo:lo + 64, :, NS + other:NS + other + 64], FAR)
                link(last)
                pool.sem_inc(g_const, 1)

            layer0(NC - 1, [clear_mask, mask_global, mask_local, mask_far])
            pool.wait_ge(wreph_ready, 1)
            nc.gpsimd.tensor_tensor(wrepl[:, :, :, :], wrep[:, :, :, :], wreph[:, :, :, :].bitcast(F32),
                                    ALU.subtract).then_inc(wrepl_ready, 1)
            def layer1(w, kind, ahead, g, i):
                if kind == "X":
                    misc_read(pool, w)
                    pool.sem_inc(apart, 1)
                    half = slice(i * C, (i + 1) * C)
                    nc.gpsimd.tensor_tensor(xn2l[:, half], xn2T[:, half], xn2h[:, half].bitcast(F32),
                                            ALU.subtract).then_inc(xn2l_ready, 1)
                elif kind == "K":
                    k, n = i // 2, w.before["K"] % 2
                    misc_read(pool, w)
                    dst = ks[:, g % 2, :] if k else qs
                    pool.sem_inc(apart, 1)
                    if i == 0:
                        pool.wait_ge(q_rows, w.no("K", 4) * 64 + 64)
                        pool.sem_inc(apart, 1)
                    nc.gpsimd.tensor_tensor(dst[:, (i % 2) * C:(i % 2 + 1) * C], kt[:, n, :],
                                            hp[:, n, :].bitcast(F32), ALU.subtract).then_inc(qk_ready, 1)

            Walk().run(pool, layer1)

        @block.vector
        def _(dve):
            dve.sem_inc(r_dve, 4)
            dve.sem_inc(h_used, 2)
            dve.sem_inc(y_used, 2)
            dve.sem_inc(a_used, len(AB))
            dve.sem_inc(m_used[0], 1)
            dve.sem_inc(m_used[1], 1)
            link = Chain(dve, d_chain)
            V = nc.vector

            def layer_norm(turn):
                even, odd = stats[:, :, 1], stats[:, :, 4]
                mean, var, sd, s0, s1, rstd = (ln[:, k, :] for k in (0, 1, 2, 3, 4, 5))
                V.tensor_tensor(s0, even, odd, ALU.add)
                V.tensor_tensor(s1, even, odd, ALU.subtract)
                link(V.tensor_tensor(var, stats[:, :, 2], stats[:, :, 5], ALU.add))
                V.tensor_scalar(mean, s0, 0.5, None, ALU.mult)
                V.tensor_scalar(var, var, 1.0 / D, EPS, ALU.mult, ALU.add)
                link(V.tensor_tensor(s1, s1, s1, ALU.mult))
                V.scalar_tensor_tensor(out=var, in0=s1, scalar=0.25, in1=var, op0=ALU.mult, op1=ALU.add).then_inc(var_ready, 1)
                dve.wait_ge(sq_ready, turn)
                link(V.reciprocal(rstd, sd))
                link(V.tensor_tensor(s0, rstd, rstd, ALU.mult))
                link(V.tensor_tensor(s0, s0, var, ALU.mult))
                link(V.tensor_scalar(s0, s0, -0.5, 1.5, ALU.mult, ALU.add))
                link(V.tensor_tensor(rstd, rstd, s0, ALU.mult))

            def normalise(tile, g):
                for t in range(4):
                    last = V.tensor_scalar(xst[:, g, t, :], x[:, tile(4 * g + t), :].rearrange("p a d -> p (a d)"),
                                           ln[:, 0, tile(4 * g + t)], ln[:, 5, tile(4 * g + t)],
                                           ALU.subtract, ALU.mult)
                last.then_inc(xn_ready, 1)

            for b in range(B):
                dve.wait_ge(x_in[b], 16)
                for t in range(b * TB, (b + 1) * TB):
                    V.bn_stats(stats[:, t, :], x[:, t, :])
            link(V.memset(al[:, 2:3], 1.0))
            layer_norm(1)
            dve.wait_ge(g_const, 1)

            def running_sum(b):
                dve.wait_ge(xT_used, 2 * b + 4)
                V.tensor_tensor_scan(z[:, b * T:(b + 1) * T], ones[:, :], xnT[:, b * T:(b + 1) * T], 0.0,
                                     ALU.mult, ALU.add).then_inc(z_sum, 1)

            for b in range(B):
                for g in range(2):
                    dve.wait_ge(xT_done, b * 2 + g + 1)
                    normalise(lambda t: slice(b * 8 + t, b * 8 + t + 1), g)
                if b:
                    running_sum(b - 1)

            dve.wait_ge(set1, 1)
            V.tensor_copy(vb_t[:, R:2 * R], bank[2][:, 0:R])
            V.tensor_copy(wb_t[:, R:2 * R], bank[2][:, R:2 * R])
            V.tensor_copy(woT[:, :], bank[2][:, 2 * R:2 * R + D])
            V.tensor_scalar(aT[:, :, :], bank[3][:, 0:2 * D].rearrange("p (k n) -> p k n", k=2), 1.0 / D, None, ALU.mult)
            V.tensor_copy(al[R:2 * R, 2:3], al[R:2 * R, 0:1])
            link(V.scalar_tensor_tensor(out=bb[:, 2:3], in0=bb[:, 0:1], scalar=al[:, 0:1], in1=bb[:, 0:1],
                                        op0=ALU.mult, op1=ALU.add))
            V.scalar_tensor_tensor(out=bb[:, 3:4], in0=bb[:, 1:2], scalar=al[:, 1:2], in1=bb[:, 2:3],
                                   op0=ALU.mult, op1=ALU.add).then_inc(set1_sb, 1)
            running_sum(B - 1)
            dve.wait_ge(lg_ps, 1)
            dve.wait_ge(early_in, 16 * 4)
            wide = [P, NT, E]
            link(V.tensor_tensor(lg[:, :, :], bank[6][:, 0:NT * E].rearrange("p (t e) -> p t e", t=NT),
                                 brb[:, :].unsqueeze(1).broadcast_to(wide), ALU.add))

            def top(logits, hot, best, tmp):
                link(V.tensor_reduce(best, logits, AX.X, ALU.max))
                link(V.tensor_tensor(hot, logits, best.unsqueeze(2).broadcast_to(wide), ALU.is_equal))
                link(V.tensor_tensor(hot, hot, desc[:, :].unsqueeze(1).broadcast_to(wide), ALU.mult))
                link(V.tensor_reduce(tmp, hot, AX.X, ALU.max))
                link(V.tensor_tensor(hot, hot, tmp.unsqueeze(2).broadcast_to(wide), ALU.is_equal))

            top(lg[:, :, :], gt[:, 0, :, :], gs[:, 0, :], gs[:, 3, :])
            link(V.scalar_tensor_tensor(out=gt[:, 1, :, :], in0=gt[:, 0, :, :], scalar=-3.0e38, in1=lg[:, :, :],
                                        op0=ALU.mult, op1=ALU.add))
            top(gt[:, 1, :, :], gt[:, 2, :, :], gs[:, 1, :], gs[:, 3, :])
            V.tensor_tensor(gs[:, 2, :], gs[:, 1, :], gs[:, 0, :], ALU.subtract).then_inc(dif_ready, 1)
            dve.wait_ge(exp_ready, 1)
            link(V.tensor_scalar(gs[:, 0, :], gs[:, 3, :], 1.0, None, ALU.add))
            link(V.reciprocal(gs[:, 1, :], gs[:, 0, :]))
            link(V.tensor_tensor(gs[:, 2, :], gs[:, 3, :], gs[:, 1, :], ALU.mult))
            V.tensor_tensor(gt[:, 0, :, :], gt[:, 0, :, :], gs[:, 1, :].unsqueeze(2).broadcast_to(wide), ALU.mult)
            link(V.tensor_tensor(gt[:, 2, :, :], gt[:, 2, :, :], gs[:, 2, :].unsqueeze(2).broadcast_to(wide), ALU.mult))
            V.tensor_tensor(w9[:, :, 1:E + 1], gt[:, 0, :, :], gt[:, 2, :, :], ALU.add).then_inc(w9_ready, 1)

            dve.wait_ge(set2, 1)
            V.tensor_copy(LQ[:, :], bank[4][:, 0:3 * R])
            V.tensor_copy(LK[:, 0:3 * R], bank[4][:, 3 * R:6 * R])
            V.tensor_copy(G[:, :], bank[4][:, 6 * R:8 * R])
            V.tensor_scalar(UB[:, :], bank[5][:, 0:D], al[:, 2:3], None, ALU.mult)
            V.tensor_scalar(UT[:, :], bank[5][0:R, D:2 * D], al[0:R, 1:2], None, ALU.mult)
            V.tensor_copy(b2a[0:1, :], bank[5][0:1, 2 * D:3 * D])
            for k in range(2):
                V.tensor_scalar(bqk_low[:, k, :], bank[5][:, 3 * D + k * HG:3 * D + (k + 1) * HG], lowm[:, k:k + 1],
                                None, ALU.mult)
            V.tensor_copy(bqk[:, :, :], bank[5][:, 3 * D:3 * D + 8].rearrange("p (k g) -> p k g", k=2)).then_inc(set2_sb, 1)

            def statistics(c):
                dve.wait_ge(yw_used, c * E + E + 2)
                for t in range(4):
                    last = V.bn_stats(stats[:, bass.ds(c * 4 + t, 1), :].rearrange("p a s -> p (a s)"),
                                      x[:, bass.ds(c * 4 + t, 1), :].rearrange("p a d -> p (a d)"))

            def layer0(c, first):
                xs = x[:, bass.ds(c * 4, 4), :]

                def weigh(e):
                    dve.wait_ge(y_ps, c * E + e + 1)
                    dve.wait_ge(yw_used, c * E + e + 1)
                    V.tensor_tensor(yw[:, e % 2, :, :], bank[4 + e % 2][:, :].rearrange("p (t d) -> p t d", t=4),
                                    w9[:, bass.ds(c * 4, 4), e + 1:e + 2].broadcast_to([P, 4, D]),
                                    ALU.mult).then_inc(y_used, 1)

                dve.wait_ge(xh_ready, c + 1)
                dve.sem_inc(apart, 1)
                V.tensor_tensor(xl[:, :], xnT[:, bass.ds(c * C, C)], xh[:, :].bitcast(F32),
                                ALU.subtract).then_inc(xl_ready, 1)
                dve.wait_ge(r_ps, c * 5 + 2)
                dve.wait_ge(r_act, c * 2 + 3)
                V.tensor_tensor(sB[:, :], sa[:, :], bank[7][:, :], ALU.mult).then_inc(r_dve, 1)
                dve.wait_ge(r_ps, c * 5 + 4)
                dve.wait_ge(r_act, c * 2 + 4)
                V.tensor_tensor(tc[:, :], sc[:, :], bank[7][0:R, :], ALU.mult).then_inc(r_dve, 1)
                dve.wait_ge(r_dve, c * 4 + 6)
                V.tensor_tensor(tri[:, :], tc[:, :], bank[7][R:2 * R, :], ALU.mult).then_inc(r_dve, 1)
                for e in range(E):
                    for j in range(2):
                        u = 2 * e + j
                        dve.wait_ge(sil_ready, c * 2 * E + u + 1)
                        V.scalar_tensor_tensor(out=actT[:, e % 2, j, :], in0=bank[2 * (u % 2) + 1][:, :],
                                               scalar=b1[:, 2 + j, e:e + 1], in1=sil[:, u % 2, :],
                                               op0=ALU.add, op1=ALU.mult).then_inc(h_used, 1)
                    if e == 0:
                        dve.wait_ge(r_ps, c * 5 + 5)
                        V.tensor_tensor(xs, xs, bank[7][:, :].rearrange("p (t d) -> p t d", t=4),
                                        ALU.add).then_inc(r_dve, 1)
                    else:
                        weigh(e - 1)
                    if e == 2 and not first:
                        statistics(c - 1)
                weigh(E - 1)

            layer0(0, True)
            with dve.Fori(1, NC) as c:
                layer0(c, False)
            V.memset(bank[6][:, :], 0.0).then_inc(o_clear, 1)
            statistics(NC - 1)

            link(V.memset(al[:, 3:4], 1.0))
            layer_norm(2)
            y_done, waited = {}, []

            def layer1(w, kind, ahead, g, i):
                if kind == "L":
                    normalise(lambda t: bass.ds((w.batch + ahead) * TB + t, 1), i)
                    return
                if kind in "AV" and not waited:
                    dve.wait_ge(g_const, 3)
                    waited.append(kind)
                if kind in "VTYF":
                    misc_full(dve, w)
                if kind in MISC:
                    misc, used = bank[MB[w.misc()]], m_used[w.misc()]
                if kind == "V":
                    lo, hi = i
                    if lo == 0:
                        dve.wait_ge(v_ready, w.no("C") + 1)
                        dve.sem_inc(apart, 1)
                    V.tensor_tensor(vnext[:, lo:hi, :, 0:HD],
                                    misc[:, 0:(hi - lo) * D].rearrange("p (j h e) -> p j h e", h=NH, e=HD),
                                    bvb[:, :].rearrange("p (h e) -> p h e", h=NH).unsqueeze(1)
                                    .broadcast_to([P, hi - lo, NH, HD]), ALU.add).then_inc(used, 1)
                elif kind == "A":
                    t, r = divmod(i, 4)
                    dve.wait_ge(a_ps, w.no("A") + 1)
                    dve.sem_inc(apart, 1)
                    V.tensor_tensor_reduce(junk[:, i % len(AB), :], bank[AB[i % len(AB)]][:, 0:KW], mask1[:, t, :], 1.0, -3.0e38,
                                           ALU.add, ALU.max, mx[:, g % 2, r, t:t + 1]).then_inc(a_used, 1)
                elif kind == "N":
                    top4 = mx[:, g % 2, :, 4 * i:4 * i + 4]
                    dve.wait_ge(a_used, w.no("A") + len(AB))
                    V.tensor_scalar(nmr[:, :, :], top4, -1.0, None, ALU.mult).then_inc(n_part, 1)
                    dve.wait_ge(n_part, w.no("N") + 1)
                    V.tensor_copy(nm[:, i, :, 0, :], nmr[:, :, :].bitcast(F32))
                    V.scalar_tensor_tensor(out=nm[:, i, :, 1, :], in0=top4, scalar=-1.0,
                                           in1=nmr[:, :, :].bitcast(F32), op0=ALU.mult,
                                           op1=ALU.subtract).then_inc(n_ready, 1)
                elif kind == "T":
                    sums = misc[:, :].rearrange("p (t r e) -> p t r e", t=4, r=4)
                    inv = rd[:, i, :].rearrange("p (t r e) -> p t r e", t=4, e=1)
                    V.reciprocal(inv, sums[:, :, :, HD:HD + 1]).then_inc(rd_ready, 1)
                    dve.wait_ge(rd_ready, w.no("T") + 1)
                    V.tensor_tensor(on[:, 4 * i:4 * i + 4, g * 32:(g + 1) * 32].rearrange("p t (r e) -> p t r e", r=4),
                                    sums[:, :, :, 0:HD], inv.broadcast_to([P, 4, 4, HD]), ALU.mult).then_inc(used, 1)
                elif kind == "Y":
                    xs = x[:, bass.ds(w.batch * TB + 4 * i, 4), :]
                    V.tensor_tensor(xs, xs, misc[:, :].rearrange("p (t d) -> p t d", t=4), ALU.add).then_inc(used, 1)
                    y_done[i] = (used, w.misc_fills() + 2)
                elif kind == "F":
                    dve.wait_ge(*y_done[i])
                    dve.wait_ge(out_done[i], w.batch * 16 + 16)
                    V.tensor_tensor(yo[:, i, :, :], x[:, bass.ds(w.batch * TB + 4 * i, 4), :],
                                    misc[:, :].rearrange("p (t d) -> p t d", t=4), ALU.add).then_inc(used, 1)

            Walk().run(dve, layer1)

        @block.tensor
        def _(pe):
            pe.sem_inc(xT_done, 2)
            pe.sem_inc(p_used, 8)

            def mm(o, l, r_, first=True, last=True, **k):
                return pe.matmul(o, l, r_, start=first, stop=last, **k)

            cos, sin, nsin = (dft[:, k, :] for k in range(3))

            def first_weights():
                pe.wait_ge(w_in, 16 * N_LOADS)
                mm(bank[2][:, 0:R], w["Winv"][:, :], wb_t[:, 0:R])
                mm(bank[2][:, R:2 * R], w["Winv"][:, :], vb_t[:, 0:R])
                pe.transpose(bank[2][:, 2 * R:2 * R + D], w["WO"][:, :], ident[:, :])
                mm(bank[3][:, 0:D], wf[:, 0, :], cos, True, False)
                mm(bank[3][:, 0:D], wf[:, 1, :], sin, False, True)
                mm(bank[3][:, D:2 * D], wf[:, 1, :], cos, True, False)
                mm(bank[3][:, D:2 * D], wf[:, 0, :], nsin, False, True).then_inc(set1, 1)

            pe.wait_ge(early_in, 16 * 4)
            for k in range(NC + 1):
                if k < NC:
                    pe.wait_ge(xn_ready, k + 1)
                    pe.wait_ge(xT_used, k + 1)
                    for t in range(4):
                        last = pe.transpose(bank[k % 2][:, t * P:(t + 1) * P], xst[:, k % 2, t, :], ident[:, :])
                    last.then_inc(xT_done, 1)
                if k:
                    pe.wait_ge(xT_used, k + 2)
                    for t in range(4 * k - 4, 4 * k):
                        last = mm(bank[6][:, t * E:(t + 1) * E], xnT[:, t * P:(t + 1) * P], Wr[:, :])
                if k == NC - 1:
                    first_weights()
            last.then_inc(lg_ps, 1)
            pe.wait_ge(set1_sb, 1)
            pe.wait_ge(g_const, 2)
            mm(bank[4][:, 0:3 * R], w["WQ"][:, :], vb_t[:, :])
            mm(bank[4][:, 3 * R:6 * R], w["WK"][:, :], wb_t[:, :])
            mm(bank[4][:, 6 * R:8 * R], aT[:, 0, :], cos, True, False)
            mm(bank[4][:, 6 * R:8 * R], aT[:, 1, :], nsin, False, True)
            mm(bank[5][:, 0:D], ub2[:, :], woT[:, :])
            mm(bank[5][0:R, D:2 * D], ut[:, :], woT[:, :])
            mm(bank[5][0:1, 2 * D:3 * D], bb[:, 3:4], woT[:, :])
            for k in range(2):
                for g in range(HG):
                    last = mm(bank[5][:, 3 * D + k * HG + g:3 * D + k * HG + g + 1],
                              brep[0:1, k, 4 * g:4 * g + 4, :].rearrange("p h e -> p (h e)"), ones[0:1, 0:1])
            last.then_inc(set2, 1)
            pe.wait_ge(w9_ready, 1)
            for k in range(NC):
                if k >= 4:
                    pe.wait_ge(w9T_ready, k - 3)
                for t in range(4):
                    last = pe.transpose(bank[k % 4][0:E + 1, t * P:(t + 1) * P], w9[:, 4 * k + t, :], ident[:, :])
                last.then_inc(w9_ps, 1)

            pe.wait_ge(set2_sb, 1)
            pe.wait_ge(z_ready, B)
            pe.wait_ge(w9T_ready, NC)
            pe.wait_ge(w1_in, 16 * 4)
            pe.wait_ge(w1l_ready, E)
            with pe.Fori(0, NC) as c:
                xc, zc = xnT[:, bass.ds(c * C, C)], z[:, bass.ds(c * C, C)]

                def hidden(e):
                    for j in range(2):
                        u = 2 * e + j
                        pe.wait_ge(h_used, c * 2 * E + u + 1)
                        for half in range(2):
                            o, cols = bank[2 * (u % 2) + half][:, :], slice(half * HF + j * P, half * HF + (j + 1) * P)
                            mm(o, W1h[:, e, cols], xh[:, :], True, False)
                            mm(o, W1h[:, e, cols], xl[:, :], False, False)
                            last = mm(o, W1l[:, e, cols], xh[:, :], False, True)
                        last.then_inc(h_ps, 1)

                def down(e):
                    pe.wait_ge(h_used, c * 2 * E + 2 * e + 4)
                    pe.wait_ge(y_used, c * E + e + 1)
                    for t in range(4):
                        for j in range(2):
                            last = mm(bank[4 + e % 2][:, t * P:(t + 1) * P], actT[:, e % 2, j, t * P:(t + 1) * P],
                                      W2[:, e, j, :], j == 0, j == 1)
                    last.then_inc(y_ps, 1)

                pe.wait_ge(r_act, c * 2 + 2)
                mm(bank[6][:, :], LQ[:, 0:2 * R], xc).then_inc(r_ps, 1)
                pe.wait_ge(r_dve, c * 4 + 4)
                mm(bank[7][:, :], LK[:, 0:2 * R], zc).then_inc(r_ps, 1)
                pe.wait_ge(r_act, c * 2 + 3)
                pe.sem_inc(apart, 1)
                mm(bank[6][0:R, :], LQ[:, 2 * R:3 * R], xc).then_inc(r_ps, 1)
                pe.wait_ge(r_dve, c * 4 + 5)
                mm(bank[7][:, :], LK[:, 2 * R:4 * R], zc).then_inc(r_ps, 1)
                pe.wait_ge(xl_ready, c + 1)
                hidden(0)
                pe.wait_ge(r_dve, c * 4 + 7)
                pe.wait_ge(w9c_ready, c + 1)
                for t in range(4):
                    s = slice(t * P, (t + 1) * P)
                    mm(bank[7][:, s], sB[:, s], UB[:, :], True, False)
                    mm(bank[7][:, s], tri[:, s], UT[:, :], False, False)
                    last = mm(bank[7][:, s], w9c[:, s], b2a[:, :], False, True)
                last.then_inc(r_ps, 1)
                for e in range(1, E):
                    hidden(e)
                    down(e - 1)
                down(E - 1)

            pe.wait_ge(identr_ready, 3)
            pe.wait_ge(h_used, NC * 2 * E + 2)
            pe.wait_ge(r_dve, NC * 4 + 4)
            pe.wait_ge(y_used, NC * E + 2)
            pe.wait_ge(o_clear, 1)
            pe.wait_ge(wrepl_ready, 1)
            pending = []

            def layer1(w, kind, ahead, g, i):
                tiles = [slice(k * P, (k + 1) * P) for k in range(4)]
                if kind in MISC:
                    pe.wait_ge(m_used[w.misc()], w.misc_fills() + 1)
                    o = bank[MB[w.misc()]]
                if kind in "VF":
                    for bank_of, fills in pending:
                        if bank_of != w.misc():
                            pe.wait_ge(m_used[bank_of], fills)
                    pending.clear()
                if kind == "X":
                    pe.wait_ge(xn_ready, w.no("X") + NC + 1)
                    for k in range(4):
                        last = pe.transpose(o[:, tiles[k]], xst[:, i, k, :], ident[:, :])
                    last.then_inc(m_ps, 1)
                    pending.append((w.misc(), w.misc_fills() + 2))
                elif kind == "V":
                    for k, j in enumerate(range(*i)):
                        rows = xn2T[:, ST - 1 + C * j:C * (j + 1):ST] if j < 2 else xn2T[:, (j - 2) * P:(j - 1) * P]
                        last = mm(o[:, tiles[k]], rows, cw[:, 2 * D:3 * D])
                    last.then_inc(m_ps, 1)
                elif kind == "K":
                    if g == 0:
                        pe.wait_ge(xn2l_ready, w.no("X") - 1 + i % 2)
                    wh, wl = (v[:, i // 2, 4 * g:4 * g + 4, :].rearrange("p h e -> p (h e)") for v in (wreph, wrepl))
                    half = slice((i % 2) * C, (i % 2 + 1) * C)
                    mm(o[:, :], wh, xn2h[:, half], True, False)
                    mm(o[:, :], wh, xn2l[:, half], False, False)
                    mm(o[:, :], wl, xn2h[:, half], False, True).then_inc(m_ps, 1)
                elif kind == "A":
                    t, r = divmod(i, 4)
                    if i == 0:
                        pe.wait_ge(qk_ready, w.no("K") + 2)
                        pe.wait_ge(q_rows, w.no("K", 4) * 64 + 64)
                    pe.wait_ge(a_used, w.no("A") + (1 if i >= 32 % len(AB) else 1 + len(AB) - 32 % len(AB)))
                    q = qz[:, g % 2, r, t * P:(t + 1) * P]
                    mm(bank[AB[i % len(AB)]][:, 0:NS], q, ks[:, g % 2, ST - 1:T:ST])
                    mm(bank[AB[i % len(AB)]][:, NS:KW], q, ks[:, g % 2, t * P:(t + 1) * P]).then_inc(a_ps, 1)
                elif kind == "M":
                    pe.wait_ge(n_ready, w.no("N"))
                    pe.sem_inc(apart, 1)
                    pe.transpose(o[0:4 * TB, 0:P], nm[:, i, :, :, :].rearrange("p r s t -> p (r s t)"),
                                 ident[:, :]).then_inc(m_ps, 1)
                elif kind == "S":
                    u = w.before["S"]
                    qc, r, part = i // 12, i % 4, PARTS[i % 12 // 4]
                    if i % 12 == 0:
                        pe.wait_ge(m_rows, w.no("M") * 64 + 64)
                    pe.wait_ge(p_ready, w.no("S") + 1)
                    o = bank[SB[u % len(SB)]]
                    q = qz[:, g % 2, r, qc * C:(qc + 1) * C]
                    if part < 2:
                        keys = ks[:, g % 2, ST - 1 + C * part:C * (part + 1):ST]
                        last = mm(o[:, :], keys, q, True, part != qc)
                        if part == qc:
                            last = mm(o[:, :], identr[:, :], mstr_r[:, :], False, True)
                    else:
                        for j, s in enumerate(tiles):
                            mm(o[:, s], ks[:, g % 2, qc * C + j * P:qc * C + (j + 1) * P], q[:, s],
                               j == 0, False, skip_group_check=True)
                        last = mm(o[:, :].rearrange("p (t k) -> p t k", t=4), identr[:, :],
                                  mloc_r[:, :].unsqueeze(1).broadcast_to([P, 4, P]), False, True,
                                  skip_group_check=True)
                    last.then_inc(s_ps, 1)
                elif kind == "P":
                    u = w.before["P"]
                    qc, r, part = i // 12, i % 4, PARTS[i % 12 // 4]
                    pe.wait_ge(p_ready, w.no("P") + 1 + len(SB))
                    if (g, i) == (0, 0):
                        pe.wait_ge(v_ready, w.no("C") + 1)
                    if i % 12 == 0:
                        pe.wait_ge(on_ready, w.no("O") + 1)
                    o = bank[6][32 * r:32 * r + HD + 1, :]
                    if part < 2:
                        last = mm(o, vaug[:, part, 4 * g + r, :], pT[:, u % 8, :], False, part == 1,
                                  skip_group_check=True)
                    else:
                        for j, s in enumerate(tiles):
                            last = mm(o[:, s], vaug[:, 2 + 4 * qc + j, 4 * g + r, :], pT[:, u % 8, s],
                                      j == 0, False, skip_group_check=True)
                    last.then_inc(p_used, 1)
                elif kind == "T":
                    pe.wait_ge(on_ready, w.no("O") + 1)
                    for s in tiles:
                        last = pe.transpose(o[:, s], onum[:, i, s], ident[:, :])
                    last.then_inc(m_ps, 1)
                    attended[i] = (w.misc(), w.misc_fills() + 2)
                elif kind == "U":
                    bank_of, fills = attended[i]
                    if bank_of != w.misc():
                        pe.wait_ge(m_used[bank_of], fills)
                    for k, s in enumerate(tiles):
                        last = pe.transpose(o[:, s], on[:, 4 * i + k, :], ident[:, :])
                    last.then_inc(m_ps, 1)
                    pending.append((w.misc(), w.misc_fills() + 2))
                elif kind == "Y":
                    for k, s in enumerate(tiles):
                        mm(o[:, s], xn2T[:, i * C + k * P:i * C + (k + 1) * P], G[:, :], True, False)
                        last = mm(o[:, s], ones[0:2, 0:P], bias2[:, :], False, True)
                    last.then_inc(m_ps, 1)
                elif kind == "F":
                    for k, s in enumerate(tiles):
                        last = mm(o[:, s], oT[:, i, s], cproj[:, :])
                    last.then_inc(m_ps, 1)

            attended = {}
            Walk().run(pe, layer1)
            assert not pending


INS = """L0_attn_x L0_attn_WQ L0_attn_WK L0_attn_WO L0_attn_Winv L0_attn_U_b L0_attn_V_b L0_attn_W_b L0_attn_bias_b
         L0_attn_U_t L0_attn_V_t L0_attn_W_t L0_attn_X_t L0_attn_bias_t L0_attn_alpha_bi L0_attn_alpha_tri
         L0_ffn_W1 L0_ffn_b1 L0_ffn_W2 L0_ffn_b2 L0_ffn_Wr L0_ffn_br
         L1_attn_c_attn_w L1_attn_c_attn_b L1_attn_c_proj_w L1_attn_c_proj_b L1_ffn_w_freq_real L1_ffn_w_freq_imag L1_ffn_bias""".split()


def constants():
    k = np.arange(D)
    angle = 2.0 * np.pi * ((k[:, None] * k[None, :]) % D) / D
    low = np.zeros((P, 2))
    low[:, 0] = k % 32 // HD == 2
    low[:, 1] = k % 32 // HD == 1
    made = {"dft": np.stack([np.cos(angle), np.sin(angle), -np.sin(angle)], 1), "low_rows": low,
            "rcount": 1.0 / np.arange(1, T + 1), "desc": np.arange(E, 0, -1), "ident": np.eye(P)}
    return {n: np.ascontiguousarray(v, np.float32) for n, v in made.items()}


def kernel(**inputs):
    import concourse.bacc as bacc
    from concourse.bass_utils import run_bass_kernel_spmd

    nc = bacc.Bacc("TRN2", target_bir_lowering=False, num_devices=1)
    arrays, args = {}, {}
    for name in INS:
        v = np.asarray(inputs[name])
        if name == "L0_ffn_b1":
            v = v.reshape(E, 2 * HF // P, P).transpose(2, 1, 0)
        arrays[name + "_dram"] = np.ascontiguousarray(v.reshape(v.shape or (1,)))
    for name, v in constants().items():
        arrays[name + "_dram"] = v
    for name, v in arrays.items():
        args[name[:-5]] = nc.dram_tensor(name, v.shape, mybir.dt.from_np(v.dtype), kind="ExternalInput").ap()
    out = nc.dram_tensor("out_dram", (B, T, D), F32, kind="ExternalOutput").ap()
    build(nc, args, out)
    got = run_bass_kernel_spmd(nc, [arrays], core_ids=[0])
    return got.results[0]["out_dram"]
```
